# Optimizing a Trainium2 kernel written in Bass

```python
import numpy as np
import jax
import jax.numpy as jnp

def _softmax(x, axis=-1):
    return jax.nn.softmax(x, axis=axis)

def _gelu(x):
    return jax.nn.gelu(x, approximate=True)

def _silu(x):
    return jax.nn.silu(x)

def _sigmoid(x):
    return jax.nn.sigmoid(x)

def _layernorm(x, axis=-1, eps=1e-05):
    m = jnp.mean(x, axis=axis, keepdims=True)
    v = jnp.var(x, axis=axis, keepdims=True)
    return (x - m) / jnp.sqrt(v + eps)

def _scatter_add(tgt, idx, src, axis=0):
    return tgt.at[idx].add(src)

def _segment_sum(src, seg, n):
    return jax.ops.segment_sum(src, seg, n)
kernel_name = 'mk_xattn_ffn_d1_seqx_r4_ccf8cf'

def setup_inputs(seed: int=0):
    np.random.seed(seed)
    _w = jnp.asarray

    def _rec_inputs():
        import jax
        import jax.numpy as jnp
        _rk = jax.random.key(seed)
        x = 4.136e-05 + 0.9999 * jax.random.normal(jax.random.fold_in(_rk, 1), (4, 512, 512), jnp.float32)
        _lenS = 512 - jax.random.randint(jax.random.fold_in(_rk, 7), (4,), 0, max(1, 512 // 4) + 1, jnp.int32)
        _lenS2 = 512 - jax.random.randint(jax.random.fold_in(_rk, 8), (4,), 0, max(1, 512 // 4) + 1, jnp.int32)
        _ctx_1024P = jax.random.normal(jax.random.fold_in(_rk, 11), (4, 16, 256), jnp.float32)
        _ctx_1024c = jax.random.dirichlet(jax.random.fold_in(_rk, 511), 0.3 * jnp.ones((16,), jnp.float32), (4, 512))
        _ctx_1024t = jnp.einsum('bsk,bkd->bsd', _ctx_1024c, _ctx_1024P)
        _ctx_1024t = _ctx_1024t * jax.lax.rsqrt(jnp.mean(jnp.square(_ctx_1024t)) + 1e-12) * 0.953939
        ctx_1024 = -0.000292821 + 1.00034 * (_ctx_1024t + 0.3 * jax.random.normal(jax.random.fold_in(_rk, 611), (4, 512, 256), jnp.float32))
        return (x, ctx_1024)
    x, ctx_1024 = _rec_inputs()

    def _L0_xattn_setup():
        import jax, jax.numpy as jnp
        import numpy as np
        import math
        B, L, DM = (2, 512, 256)
        DS, DC, EXP = (16, 4, 2)
        DI = EXP * DM
        DR = math.ceil(DM / 16)
        DT_MIN, DT_MAX, DT_FLOOR = (0.001, 0.1, 0.0001)

        def _ssm_forward(hidden_states, z, in_proj_w, conv_w, conv_b, x_proj_w, dt_proj_w, dt_proj_b, A_log, D):
            b = hidden_states.shape[0]
            x = jnp.einsum('ed,bld->bel', in_proj_w, hidden_states)
            xp = jnp.pad(x, ((0, 0), (0, 0), (DC - 1, 0)))
            xc = jax.lax.conv_general_dilated(xp, conv_w[:, None, :], window_strides=(1,), padding='VALID', dimension_numbers=('NCH', 'OIH', 'NCH'), feature_group_count=DI)
            u = jax.nn.silu(xc + conv_b[None, :, None])
            x_dbl = jnp.einsum('ke,bel->bkl', x_proj_w, u)
            dt_lo = x_dbl[:, :DR]
            Bm = x_dbl[:, DR:DR + DS]
            Cm = x_dbl[:, DR + DS:]
            delta = jax.nn.softplus(jnp.einsum('er,brl->bel', dt_proj_w, dt_lo) + dt_proj_b[None, :, None])
            A = -jnp.exp(A_log)

            def step(state, xs):
                d_t, B_t, C_t, u_t = xs
                dA = jnp.exp(d_t[..., None] * A)
                state = state * dA + (d_t * u_t)[..., None] * B_t[:, None, :]
                y_t = jnp.einsum('ben,bn->be', state, C_t)
                return (state, y_t)
            xs = (jnp.moveaxis(delta, -1, 0), jnp.moveaxis(Bm, -1, 0), jnp.moveaxis(Cm, -1, 0), jnp.moveaxis(u, -1, 0))
            state0 = jnp.zeros((b, DI, DS), delta.dtype)
            _, ys = jax.lax.scan(step, state0, xs)
            y = jnp.moveaxis(ys, 0, -1)
            y = y + D[None, :, None] * u
            y = y * jax.nn.silu(z)
            return jnp.swapaxes(y, 1, 2)
        key = jax.random.key(seed)
        ks = jax.random.split(key, 8)
        hidden_states = jax.random.normal(ks[0], (B, L, DM), jnp.float32)
        z = jax.random.normal(ks[1], (B, DI, L), jnp.float32)
        in_proj_w = jax.random.normal(ks[2], (DI, DM), jnp.float32) * DM ** (-0.5)
        conv_w = jax.random.normal(ks[3], (DI, DC), jnp.float32) * DC ** (-0.5)
        conv_b = jnp.zeros((DI,), jnp.float32)
        x_proj_w = jax.random.normal(ks[4], (DR + 2 * DS, DI), jnp.float32) * DI ** (-0.5)
        dt_std = DR ** (-0.5)
        dt_proj_w = jax.random.uniform(ks[5], (DI, DR), jnp.float32, -dt_std, dt_std)
        dt = jnp.exp(jax.random.uniform(ks[6], (DI,), jnp.float32) * (math.log(DT_MAX) - math.log(DT_MIN)) + math.log(DT_MIN))
        dt = jnp.clip(dt, DT_FLOOR)
        dt_proj_b = dt + jnp.log(-jnp.expm1(-dt))
        A_log = jnp.log(jnp.broadcast_to(jnp.arange(1, DS + 1, dtype=jnp.float32), (DI, DS)))
        D = jnp.ones((DI,), jnp.float32)
        return dict(hidden_states=hidden_states, z=z, in_proj_w=in_proj_w, conv_w=conv_w, conv_b=conv_b, x_proj_w=x_proj_w, dt_proj_w=dt_proj_w, dt_proj_b=dt_proj_b, A_log=A_log, D=D)
    _L0_xattn_all = _L0_xattn_setup()
    _L0_xattn_in = {k: v for k, v in _L0_xattn_all.items() if k in ('in_proj_w', 'conv_w', 'conv_b', 'x_proj_w', 'dt_proj_w', 'dt_proj_b', 'A_log', 'D')}
    del _L0_xattn_all

    def _L0_ffn_setup():
        import jax, jax.numpy as jnp
        import numpy as np
        DIM_IN = 512
        DIM_HIDDEN = 2048
        key = jax.random.key(seed)
        k_x, k_g, k_u, k_d = jax.random.split(key, 4)
        s_in = 1.0 / np.sqrt(DIM_IN)
        s_hid = 1.0 / np.sqrt(DIM_HIDDEN)
        x = jax.random.normal(k_x, (4, 512, DIM_IN), dtype=jnp.float32)
        w_gate = jax.random.uniform(k_g, (DIM_HIDDEN, DIM_IN), jnp.float32, -s_in, s_in)
        w_up = jax.random.uniform(k_u, (DIM_HIDDEN, DIM_IN), jnp.float32, -s_in, s_in)
        w_down = jax.random.uniform(k_d, (DIM_IN, DIM_HIDDEN), jnp.float32, -s_hid, s_hid)
        return {'x': x, 'w_gate': w_gate, 'w_up': w_up, 'w_down': w_down}
    _L0_ffn_all = _L0_ffn_setup()
    _L0_ffn_in = {k: v for k, v in _L0_ffn_all.items() if k in ('w_gate', 'w_up', 'w_down')}
    del _L0_ffn_all
    return {'x': x, 'ctx_1024': ctx_1024, 'L0_xattn_in_proj_w': _L0_xattn_in['in_proj_w'], 'L0_xattn_conv_w': _L0_xattn_in['conv_w'], 'L0_xattn_conv_b': _L0_xattn_in['conv_b'], 'L0_xattn_x_proj_w': _L0_xattn_in['x_proj_w'], 'L0_xattn_dt_proj_w': _L0_xattn_in['dt_proj_w'], 'L0_xattn_dt_proj_b': _L0_xattn_in['dt_proj_b'], 'L0_xattn_A_log': _L0_xattn_in['A_log'], 'L0_xattn_D': _L0_xattn_in['D'], 'L0_ffn_w_gate': _L0_ffn_in['w_gate'], 'L0_ffn_w_up': _L0_ffn_in['w_up'], 'L0_ffn_w_down': _L0_ffn_in['w_down']}

def reference(x, ctx_1024, L0_xattn_in_proj_w, L0_xattn_conv_w, L0_xattn_conv_b, L0_xattn_x_proj_w, L0_xattn_dt_proj_w, L0_xattn_dt_proj_b, L0_xattn_A_log, L0_xattn_D, L0_ffn_w_gate, L0_ffn_w_up, L0_ffn_w_down):
    import jax
    import jax.numpy as jnp

    def _L0_xattn_ref(hidden_states, z, in_proj_w, conv_w, conv_b, x_proj_w, dt_proj_w, dt_proj_b, A_log, D):
        import jax, jax.numpy as jnp
        import numpy as np
        import math
        B, L, DM = (2, 512, 256)
        DS, DC, EXP = (16, 4, 2)
        DI = EXP * DM
        DR = math.ceil(DM / 16)
        DT_MIN, DT_MAX, DT_FLOOR = (0.001, 0.1, 0.0001)

        def _ssm_forward(hidden_states, z, in_proj_w, conv_w, conv_b, x_proj_w, dt_proj_w, dt_proj_b, A_log, D):
            b = hidden_states.shape[0]
            x = jnp.einsum('ed,bld->bel', in_proj_w, hidden_states)
            xp = jnp.pad(x, ((0, 0), (0, 0), (DC - 1, 0)))
            xc = jax.lax.conv_general_dilated(xp, conv_w[:, None, :], window_strides=(1,), padding='VALID', dimension_numbers=('NCH', 'OIH', 'NCH'), feature_group_count=DI)
            u = jax.nn.silu(xc + conv_b[None, :, None])
            x_dbl = jnp.einsum('ke,bel->bkl', x_proj_w, u)
            dt_lo = x_dbl[:, :DR]
            Bm = x_dbl[:, DR:DR + DS]
            Cm = x_dbl[:, DR + DS:]
            delta = jax.nn.softplus(jnp.einsum('er,brl->bel', dt_proj_w, dt_lo) + dt_proj_b[None, :, None])
            A = -jnp.exp(A_log)

            def step(state, xs):
                d_t, B_t, C_t, u_t = xs
                dA = jnp.exp(d_t[..., None] * A)
                state = state * dA + (d_t * u_t)[..., None] * B_t[:, None, :]
                y_t = jnp.einsum('ben,bn->be', state, C_t)
                return (state, y_t)
            xs = (jnp.moveaxis(delta, -1, 0), jnp.moveaxis(Bm, -1, 0), jnp.moveaxis(Cm, -1, 0), jnp.moveaxis(u, -1, 0))
            state0 = jnp.zeros((b, DI, DS), delta.dtype)
            _, ys = jax.lax.scan(step, state0, xs)
            y = jnp.moveaxis(ys, 0, -1)
            y = y + D[None, :, None] * u
            y = y * jax.nn.silu(z)
            return jnp.swapaxes(y, 1, 2)
        return _ssm_forward(hidden_states, z, in_proj_w, conv_w, conv_b, x_proj_w, dt_proj_w, dt_proj_b, A_log, D)

    def _L0_ffn_ref(x, w_gate, w_up, w_down):
        import jax, jax.numpy as jnp
        import numpy as np
        DIM_IN = 512
        DIM_HIDDEN = 2048
        gate = jnp.einsum('bsd,hd->bsh', x, w_gate)
        up = jnp.einsum('bsd,hd->bsh', x, w_up)
        gated = jax.nn.silu(gate) * up
        return jnp.einsum('bsh,dh->bsd', gated, w_down)
    x = x + _L0_xattn_ref(ctx_1024, _layernorm(x, axis=-1), L0_xattn_in_proj_w, L0_xattn_conv_w, L0_xattn_conv_b, L0_xattn_x_proj_w, L0_xattn_dt_proj_w, L0_xattn_dt_proj_b, L0_xattn_A_log, L0_xattn_D)
    x = x + _L0_ffn_ref(_layernorm(x, axis=-1), L0_ffn_w_gate, L0_ffn_w_up, L0_ffn_w_down)
    return x

_drawn_inputs = setup_inputs


def setup_inputs(seed=0):
    import zlib

    import numpy as np

    out = dict(_drawn_inputs(seed))
    spreads = {'L0_xattn_conv_b': (0.0, 0.1), 'L0_xattn_D': (1.0, 0.2)}
    factors = {'L0_xattn_dt_proj_w': 5.229}
    for name, (base, spread) in spreads.items():
        noise = np.random.default_rng([zlib.crc32(name.encode()), seed]).standard_normal(out[name].shape)
        drawn = base * np.exp(spread * noise) if base else spread * noise
        out[name] = jnp.asarray(drawn.astype(out[name].dtype))
    for name, factor in factors.items():
        out[name] = (out[name] * factor).astype(out[name].dtype)
    return out
```

```python
from contextlib import ExitStack

import numpy as np
import concourse.bass as bass
from concourse import mybir

P = 128
BATCH, SEQ, DIM = 4, 512, 512
CTX = 256
CHAN = 512
NST = 16
TAPS = 4
RANK = 16
HID = 2048
EPS = 1e-5

L = 256
HALVES = SEQ // L
UNITS = BATCH * HALVES
ET = CHAN // P
CT = CTX // P
DT = DIM // P
TT = L // P
SLOTS = 8
LAG = 2
XBUF = 4
PAD = L + 1

F32 = mybir.dt.float32
ALU = mybir.AluOpType
ACT = mybir.ActivationFunctionType


def wait(eng, sem, count):
    if not isinstance(count, int) or count > 0:
        eng.wait_ge(sem, count)


def build(nc, ctx_t, x, w_in, conv_w, conv_b, w_x, w_dt, dt_b, a_log, d_skip, w_gate, w_up, w_down, out):
    x_chan = x.rearrange("b (e p) t -> b p e t", p=P)
    x_tok = x.rearrange("b (h t p) d -> (b h) p t d", p=P, t=TT)
    out_tok = out.rearrange("b (h t p) d -> (b h) p t d", p=P, t=TT)
    bc_rows = nc.dram_tensor("bc_rows", (UNITS, 2, NST, L), F32, kind="Internal").ap()

    with ExitStack() as stack:
        def sb(name, shape):
            return stack.enter_context(nc.sbuf_tensor(name, shape, F32))

        def sem(name):
            return stack.enter_context(nc.semaphore(name))

        wg = sb("wg", [P, DT, HID])
        wu = sb("wu", [P, DT, HID])
        wd = sb("wd", [P, HID // P, DIM])
        win = sb("win", [P, CT, CHAN])
        wx = sb("wx", [P, ET, RANK + 2 * NST])
        wdt = sb("wdt", [RANK, CHAN])
        cw = sb("cw", [P, ET, TAPS])
        cb = sb("cb", [P, ET])
        dtb = sb("dtb", [P, ET])
        decay = sb("decay", [P, ET, NST])
        dhalf = sb("dhalf", [P, ET])
        ident = sb("ident", [P, P])
        neghalf = sb("neghalf", [P, ET])
        epsilon = sb("epsilon", [P, ET])

        ctxs = sb("ctxs", [P, CT, L])
        xch = sb("xch", [P, ET, DIM])
        xin = sb("xin", [P, ET, TAPS - 1 + L])
        nohead = sb("nohead", [P, ET, TAPS - 1])
        u2 = sb("u2", [P, ET, L])
        tmp = sb("tmp", [P, ET, L])
        zs = sb("zs", [P, ET, L])
        xdbl = sb("xdbl", [RANK + 2 * NST, L])
        delta = [sb(f"delta{h}", [P, ET, L]) for h in range(2)]
        du = [sb(f"du{h}", [P, ET, L]) for h in range(2)]
        gate = [sb(f"gate{h}", [P, ET, L]) for h in range(2)]
        acc = [sb(f"acc{h}", [P, ET, L]) for h in range(2)]
        x2 = [sb(f"x2{h}", [P, TT, DIM]) for h in range(2)]
        da = [sb(f"da{i}", [P, ET, PAD]) for i in range(2)]
        st = [sb(f"st{i}", [P, ET, PAD]) for i in range(XBUF)]
        carry = sb("carry", [P, NST, ET])
        bc = [sb(f"bc{i}", [P, 2, 2, L]) for i in range(2)]
        xht = sb("xht", [P, DT, L])
        th = [sb(f"th{i}", [P, 2 * L]) for i in range(2)]
        gu = [sb(f"gu{i}", [P, 2 * L]) for i in range(2)]
        waiter = sb("waiter", [P, 1])
        zst = sb("zst", [P, ET, 6])
        zmv = sb("zmv", [P, ET, 2])
        zr = sb("zr", [P, ET])
        znb = sb("znb", [P, ET])
        yst = sb("yst", [P, TT, 6])
        ymv = sb("ymv", [P, TT, 2])
        yr = sb("yr", [P, TT])
        ynb = sb("ynb", [P, TT])

        ps_gate = [stack.enter_context(nc.psum_tensor(f"ps_gate{i}", [P, 2 * L], F32)) for i in range(2)]
        ps_up = [stack.enter_context(nc.psum_tensor(f"ps_up{i}", [P, 2 * L], F32)) for i in range(2)]
        ps_down = [stack.enter_context(nc.psum_tensor(f"ps_down{i}", [P, DIM], F32)) for i in range(TT)]
        ps_misc = [stack.enter_context(nc.psum_tensor(f"ps_misc{i}", [P, 2 * L], F32)) for i in range(2)]

        small_loaded = sem("small_loaded")
        wg_loaded = sem("wg_loaded")
        wu_loaded = sem("wu_loaded")
        wd_loaded = sem("wd_loaded")
        ctx_loaded = sem("ctx_loaded")
        xch_loaded = sem("xch_loaded")
        x2_loaded = sem("x2_loaded")
        rows_stored = sem("rows_stored")
        bc_loaded = [sem(f"bc_loaded{i}") for i in range(2)]
        out_stored = sem("out_stored")
        consts_made = sem("consts_made")
        decay_made = sem("decay_made")
        zeros_made = sem("zeros_made")
        proj_done = sem("proj_done")
        xdbl_done = sem("xdbl_done")
        dt_done = sem("dt_done")
        yt_done = sem("yt_done")
        xht_done = sem("xht_done")
        gate_done = sem("gate_done")
        up_done = sem("up_done")
        down_done = sem("down_done")
        xin_ready = sem("xin_ready")
        head_ready = sem("head_ready")
        uth_ready = sem("uth_ready")
        xdbl_ready = sem("xdbl_ready")
        dt_read = sem("dt_read")
        soft_step = sem("soft_step")
        z_ready = sem("z_ready")
        zth_ready = sem("zth_ready")
        acc_started = sem("acc_started")
        decays_ready = sem("decays_ready")
        xh_ready = sem("xh_ready")
        xht_ready = sem("xht_ready")
        tanh_ready = sem("tanh_ready")
        conv_started = sem("conv_started")
        conv_step = sem("conv_step")
        rstd_step = sem("rstd_step")
        yrstd_step = sem("yrstd_step")
        scaled = sem("scaled")
        u_ready = sem("u_ready")
        delta_ready = sem("delta_ready")
        du_ready = sem("du_ready")
        stats_step = sem("stats_step")
        znb_ready = sem("znb_ready")
        zgate_ready = sem("zgate_ready")
        seeded = sem("seeded")
        input_ready = sem("input_ready")
        scanned = sem("scanned")
        saved = sem("saved")
        added = sem("added")
        yg_ready = sem("yg_ready")
        x2_ready = sem("x2_ready")
        ystats_step = sem("ystats_step")
        ynb_ready = sem("ynb_ready")
        silu_ready = sem("silu_ready")
        gu_ready = sem("gu_ready")
        out_ready = sem("out_ready")

        block = stack.enter_context(nc.Block())

        def schedule(eng, unit):
            unit(0, 0, False)
            unit(0, 1, False)
            unit(1, 0, False)
            with eng.Fori(0, BATCH - 2) as i:
                unit(i + 1, 1, True)
                unit(i + 2, 0, True)
            unit(BATCH - 1, 1, False)
            unit(BATCH, 0, False)
            unit(BATCH, 1, False)

        def parts(u, inside, jp):
            scans = inside or u < UNITS
            prepares = inside or u < UNITS - 1
            w, q = (u - 1, jp - LAG) if jp >= LAG else (u - 2, SLOTS - LAG + jp)
            feeds = inside or 0 <= w < UNITS
            return scans, prepares, (w, q) if feeds else None

        @block.sync
        def _(sp):
            def load_ctx(u):
                wait(sp, proj_done, 2 * u)
                sp.dma_start(ctxs[:], ctx_t[bass.ds(u, 1)].rearrange("o p c t -> (o p) c t")).then_inc(ctx_loaded, 16)

            def load_xch(b):
                wait(sp, z_ready, HALVES * b)
                sp.dma_start(xch[:], x_chan[bass.ds(b, 1)].rearrange("o p e t -> (o p) e t")).then_inc(xch_loaded, 16)

            def load_x2(u, h):
                wait(sp, out_stored, 16 * (u - 1))
                sp.dma_start(x2[h][:], x_tok[bass.ds(u, 1)].rearrange("o p t d -> (o p) t d")).then_inc(x2_loaded, 16)

            def load_bc(u, jp):
                if jp == 0:
                    sp.wait_ge(rows_stored, 16 * (u + 1))
                wait(sp, input_ready, NST * u + 2 * (jp - 1))
                wait(sp, scaled, NST * u + 2 * (jp - 1))
                src = bc_rows[bass.ds(u, 1), :, 2 * jp:2 * jp + 2, :].rearrange("o a n t -> o a (n t)")
                sp.dma_start(bc[jp % 2][:].rearrange("p a n t -> p a (n t)"),
                             src.broadcast_to([P, 2, 2 * L])).then_inc(bc_loaded[jp % 2], 16)

            def store_rows(u):
                sp.wait_ge(xdbl_ready, u + 1)
                sp.dma_start(bc_rows[bass.ds(u, 1)].rearrange("o a n t -> (o a n) t"),
                             xdbl[RANK:, :]).then_inc(rows_stored, 16)

            def store_out(w, h):
                sp.wait_ge(out_ready, 2 * (w + 1))
                sp.dma_start(out_tok[bass.ds(w, 1)].rearrange("o p t d -> (o p) t d"), x2[h][:]).then_inc(out_stored, 16)

            load_ctx(0)
            for dst, src in ((win, w_in), (cw, conv_w), (cb, conv_b), (dtb, dt_b), (decay, a_log), (dhalf, d_skip),
                             (wx, w_x), (wdt, w_dt)):
                sp.dma_start(dst[:], src).then_inc(small_loaded, 16)
            load_xch(0)
            store_rows(0)
            load_bc(0, 0)
            load_bc(0, 1)
            load_x2(0, 0)
            load_x2(1, 1)
            sp.dma_start(wg[:], w_gate).then_inc(wg_loaded, 16)
            sp.dma_start(wu[:], w_up).then_inc(wu_loaded, 16)
            sp.dma_start(wd[:], w_down).then_inc(wd_loaded, 16)

            def unit(b, h, inside):
                u = HALVES * b + h
                for jp in range(SLOTS):
                    scans, prepares, ffn = parts(u, inside, jp)
                    if prepares and jp == 0:
                        load_ctx(u + 1)
                        if h == 1:
                            load_xch(b + 1)
                    if scans and jp < SLOTS - 2:
                        load_bc(u, jp + 2)
                    if ffn and ffn[1] == 1:
                        if inside or u >= 2:
                            store_out(u - 2, h)
                        if scans and (inside or u >= 2):
                            load_x2(u, h)
                    if prepares and jp == 4:
                        store_rows(u + 1)
                    if prepares and jp >= SLOTS - 2:
                        load_bc(u + 1, jp - (SLOTS - 2))
            schedule(sp, unit)
            store_out(UNITS - 1, (UNITS - 1) % 2)
            sp.wait_ge(rows_stored, 16 * UNITS)
            sp.wait_ge(out_stored, 16 * UNITS)

        @block.tensor
        def _(pe):
            def project_in(u):
                pe.wait_ge(ctx_loaded, 16 * (u + 1))
                wait(pe, dt_read, 2 * u)
                wait(pe, xht_ready, 2 * (u - 1))
                for et in range(ET):
                    for c in range(CT):
                        mm = nc.tensor.matmul(ps_misc[et // 2][:, (et % 2) * L:(et % 2 + 1) * L],
                                              win[:, c, et * P:(et + 1) * P], ctxs[:, c, :],
                                              start=(c == 0), stop=(c == CT - 1))
                    if et % 2 == 1:
                        mm.then_inc(proj_done, 1)

            def project_x(u):
                pe.wait_ge(u_ready, u + 1)
                pe.wait_ge(xin_ready, 2 * u + 1)
                for et in range(ET):
                    mm = nc.tensor.matmul(ps_misc[0][0:RANK + 2 * NST, 0:L], wx[:, et, :], u2[:, et, :],
                                          start=(et == 0), stop=(et == ET - 1))
                mm.then_inc(xdbl_done, 1)

            def project_dt(u):
                pe.wait_ge(xin_ready, 2 * u + 2)
                pe.wait_ge(xdbl_ready, u + 1)
                for et in range(ET):
                    mm = nc.tensor.matmul(ps_misc[1 - et // 2][:, (et % 2) * L:(et % 2 + 1) * L],
                                          wdt[:, et * P:(et + 1) * P], xdbl[0:RANK, :], start=True, stop=True)
                    if et % 2 == 1:
                        mm.then_inc(dt_done, 1)

            def transpose_y(u, h, prepared):
                pe.wait_ge(yg_ready, u + 1)
                pe.wait_ge(dt_read, 2 * (u + 2) if prepared else 2 * (u + 1))
                wait(pe, xht_ready, 2 * u)
                for t in range(TT):
                    for et in range(ET):
                        mm = nc.tensor.transpose(ps_misc[t][:, et * P:(et + 1) * P], gate[h][:, et, t * P:(t + 1) * P],
                                                 ident[:])
                    mm.then_inc(yt_done, 1)

            def transpose_norm(u, h):
                rows = gate[h][:].rearrange("p e t -> p (e t)").rearrange("p (t d) -> p t d", t=TT)
                for t in range(TT):
                    pe.wait_ge(xh_ready, 2 * u + t + 1)
                    for k in range(DT):
                        mm = nc.tensor.transpose(ps_misc[t][:, k * P:(k + 1) * P], rows[:, t, k * P:(k + 1) * P],
                                                 ident[:])
                    mm.then_inc(xht_done, 1)

            def down(w, q):
                p = SLOTS * w + q
                pe.wait_ge(gu_ready, p + 1)
                if q == 0:
                    wait(pe, out_ready, 2 * w)
                for t in range(TT):
                    for j in range(2):
                        mm = nc.tensor.matmul(ps_down[t][:], gu[q % 2][:, j * L + t * P:j * L + (t + 1) * P],
                                              wd[:, 2 * q + j, :], start=(q == 0 and j == 0),
                                              stop=(q == SLOTS - 1 and j == 1))
                mm.then_inc(down_done, 1)

            def feed(w, q, first):
                p = SLOTS * w + q
                if q == 0:
                    if not first:
                        down(w - 1, SLOTS - 1)
                    pe.wait_ge(xht_ready, 2 * (w + 1))
                for ps, weights, free, done in ((ps_gate, wg, silu_ready, gate_done), (ps_up, wu, gu_ready, up_done)):
                    wait(pe, free, p - 1)
                    for j in range(2):
                        tile = 2 * q + j
                        for k in range(DT):
                            mm = nc.tensor.matmul(ps[q % 2][:, j * L:(j + 1) * L], weights[:, k, tile * P:(tile + 1) * P],
                                                  xht[:, k, :], start=(k == 0), stop=(k == DT - 1))
                    mm.then_inc(done, 1)
                if q > 0:
                    down(w, q - 1)

            pe.wait_ge(small_loaded, 16 * 8)
            project_in(0)
            project_x(0)
            project_dt(0)
            pe.wait_ge(consts_made, 4)

            def unit(b, h, inside):
                u = HALVES * b + h
                for jp in range(SLOTS):
                    scans, prepares, ffn = parts(u, inside, jp)
                    if ffn:
                        first = not inside and ffn[0] == 0
                        if first and ffn[1] == 0:
                            pe.wait_ge(wg_loaded, 16)
                            pe.wait_ge(wu_loaded, 16)
                            pe.wait_ge(wd_loaded, 16)
                        feed(ffn[0], ffn[1], first)
                    if jp == LAG - 1 and (inside or 0 < u <= UNITS):
                        transpose_norm(u - 1, 1 - h)
                    if prepares and jp == 2:
                        project_in(u + 1)
                    if prepares and jp == 4:
                        project_x(u + 1)
                    if prepares and jp == 5:
                        project_dt(u + 1)
                if scans:
                    transpose_y(u, h, prepares)
            schedule(pe, unit)
            down(UNITS - 1, SLOTS - 1)

        @block.scalar
        def _(act):
            def take_in(u, h):
                wait(act, conv_step, (TAPS - 1) * u)
                nc.scalar.activation(xin[:, :, 0:TAPS - 1], xin[:, :, L:L + TAPS - 1] if h else nohead[:],
                                     ACT.Copy).then_inc(head_ready, 1)
                act.wait_ge(head_ready, u + 1)
                for i in range(2):
                    act.wait_ge(proj_done, 2 * u + i + 1)
                    nc.scalar.activation(xin[:, 2 * i:2 * i + 2, TAPS - 1:],
                                         ps_misc[i][:].rearrange("p (e t) -> p e t", e=2), ACT.Copy).then_inc(xin_ready, 1)

            def start_conv(u):
                act.wait_ge(xin_ready, 2 * (u + 1))
                wait(act, xdbl_done, u)
                wait(act, du_ready, u)
                wait(act, acc_started, u)
                for et in range(ET):
                    a = nc.scalar.activation(u2[:, et, :], xin[:, et, 0:L], ACT.Identity, scale=cw[:, et, 0:1],
                                             bias=cb[:, et:et + 1])
                a.then_inc(conv_started, 1)

            def tanh_u(u):
                act.wait_ge(conv_step, (TAPS - 1) * (u + 1))
                wait(act, delta_ready, u)
                nc.scalar.activation(tmp[:], u2[:], ACT.Tanh, scale=0.5).then_inc(uth_ready, 1)

            def norm_z(u, h, b):
                act.wait_ge(znb_ready, b + 1)
                wait(act, zgate_ready, u)
                for et in range(ET):
                    a = nc.scalar.activation(zs[:, et, :], xch[:, et, h * L:(h + 1) * L], ACT.Identity,
                                             scale=zr[:, et:et + 1], bias=znb[:, et:et + 1])
                a.then_inc(z_ready, 1)

            def tanh_z(u):
                act.wait_ge(z_ready, u + 1)
                act.wait_ge(u_ready, u + 1)
                nc.scalar.activation(tmp[:], zs[:], ACT.Tanh, scale=0.5).then_inc(zth_ready, 1)

            def take_rows(u):
                act.wait_ge(xdbl_done, u + 1)
                wait(act, rows_stored, 16 * u)
                wait(act, dt_done, 2 * u)
                nc.scalar.activation(xdbl[:], ps_misc[0][0:RANK + 2 * NST, 0:L], ACT.Copy, scale=0.5).then_inc(xdbl_ready, 1)

            def soften(u, h):
                act.wait_ge(zgate_ready, u + 1)
                for et in range(ET):
                    if et % 2 == 0:
                        act.wait_ge(dt_done, 2 * u + et // 2 + 1)
                    src = ps_misc[1 - et // 2][:, (et % 2) * L:(et % 2 + 1) * L]
                    nc.scalar.activation(delta[h][:, et, :], src, ACT.Relu, bias=dtb[:, et:et + 1])
                    a = nc.scalar.activation(tmp[:, et, :], src, ACT.Abs, bias=dtb[:, et:et + 1])
                    if et % 2 == 1:
                        a.then_inc(dt_read, 1)
                act.wait_ge(dt_read, 2 * (u + 1))
                nc.scalar.activation(tmp[:], tmp[:], ACT.Exp, scale=-1.0).then_inc(soft_step, 1)
                act.wait_ge(soft_step, 2 * u + 1)
                nc.scalar.activation(tmp[:], tmp[:], ACT.Ln, bias=1.0).then_inc(soft_step, 1)

            def start_acc(u, h):
                act.wait_ge(u_ready, u + 1)
                wait(act, yg_ready, u - 1)
                for et in range(ET):
                    a = nc.scalar.activation(acc[h][:, et, :], u2[:, et, :], ACT.Copy, scale=dhalf[:, et:et + 1])
                a.then_inc(acc_started, 1)

            def decays(u, h, n):
                if n == 0:
                    act.wait_ge(delta_ready, u + 1)
                wait(act, scanned, NST * u + n - 1)
                for et in range(ET):
                    a = nc.scalar.activation(da[n % 2][:, et, 1:], delta[h][:, et, :], ACT.Exp,
                                             scale=decay[:, et, n:n + 1])
                a.then_inc(decays_ready, 1)

            def tanh_gate(w, q):
                p = SLOTS * w + q
                act.wait_ge(gate_done, p + 1)
                wait(act, gu_ready, p - 1)
                nc.scalar.activation(th[q % 2][:], ps_gate[q % 2][:], ACT.Tanh, scale=0.5).then_inc(tanh_ready, 1)

            def norm_y(u, h):
                act.wait_ge(ynb_ready, u + 1)
                act.wait_ge(yt_done, 2 * (u + 1))
                rows = gate[h][:].rearrange("p e t -> p (e t)").rearrange("p (t d) -> p t d", t=TT)
                for t in range(TT):
                    nc.scalar.activation(rows[:, t, :], x2[h][:, t, :], ACT.Identity, scale=yr[:, t:t + 1],
                                         bias=ynb[:, t:t + 1]).then_inc(xh_ready, 1)

            def take_norm(u):
                wait(act, up_done, SLOTS * u)
                for t in range(TT):
                    act.wait_ge(xht_done, 2 * u + t + 1)
                    nc.scalar.activation(xht[:, :, t * P:(t + 1) * P],
                                         ps_misc[t][:].rearrange("p (k l) -> p k l", k=DT), ACT.Copy).then_inc(xht_ready, 1)

            act.wait_ge(small_loaded, 16 * 8)
            nc.scalar.activation(decay[:], decay[:], ACT.Exp).then_inc(decay_made, 1)
            act.wait_ge(decay_made, 1)
            nc.scalar.activation(decay[:], decay[:], ACT.Copy, scale=-1.0).then_inc(decay_made, 1)
            nc.scalar.activation(dhalf[:], dhalf[:], ACT.Copy, scale=0.5).then_inc(decay_made, 1)
            act.wait_ge(zeros_made, 3)
            act.wait_ge(decay_made, 3)
            take_in(0, 0)
            start_conv(0)
            norm_z(0, 0, 0)
            tanh_u(0)
            tanh_z(0)
            take_rows(0)
            soften(0, 0)
            start_acc(0, 0)
            decays(0, 0, 0)

            def unit(b, h, inside):
                u = HALVES * b + h
                for jp in range(SLOTS):
                    scans, prepares, ffn = parts(u, inside, jp)
                    if scans:
                        decays(u, h, 2 * jp + 1)
                    if ffn:
                        tanh_gate(*ffn)
                    if scans and jp < SLOTS - 1:
                        decays(u, h, 2 * jp + 2)
                    elif prepares and jp == SLOTS - 1:
                        decays(u + 1, 1 - h, 0)
                    if jp == 0 and (inside or 0 < u <= UNITS):
                        norm_y(u - 1, 1 - h)
                    if jp == LAG - 1 and (inside or 0 < u <= UNITS):
                        take_norm(u - 1)
                    if prepares:
                        if jp == 2:
                            take_in(u + 1, 1 - h)
                            start_conv(u + 1)
                        if jp == 3:
                            norm_z(u + 1, 1 - h, b + h)
                            tanh_u(u + 1)
                        if jp == 4:
                            tanh_z(u + 1)
                            take_rows(u + 1)
                        if jp == 5:
                            soften(u + 1, 1 - h)
                        if jp == 6:
                            start_acc(u + 1, 1 - h)
            schedule(act, unit)

        @block.gpsimd
        def _(pool):
            def rstd_z(b):
                pool.wait_ge(stats_step, 2 * (b + 1))
                wait(pool, z_ready, HALVES * b)
                nc.gpsimd.tensor_tensor(zr[:], zmv[:, :, 1], epsilon[:], ALU.add).then_inc(rstd_step, 1)
                pool.wait_ge(rstd_step, 2 * b + 1)
                nc.gpsimd.tensor_tensor(zr[:], zr[:], neghalf[:], ALU.pow).then_inc(rstd_step, 1)

            def rstd_y(u):
                pool.wait_ge(ystats_step, 2 * (u + 1))
                wait(pool, xh_ready, 2 * u)
                nc.gpsimd.tensor_tensor(yr[:], ymv[:, :, 1], epsilon[:, 0:TT], ALU.add).then_inc(yrstd_step, 1)
                pool.wait_ge(yrstd_step, 2 * u + 1)
                nc.gpsimd.tensor_tensor(yr[:], yr[:], neghalf[:, 0:TT], ALU.pow).then_inc(yrstd_step, 1)

            def scale(u, h, b, n):
                if n % 2 == 0:
                    pool.wait_ge(bc_loaded[n // 2 % 2], 16 * (SLOTS // 2 * u + n // 4 + 1))
                pool.wait_ge(scanned, NST * u + n + 1)
                if h == 0:
                    pool.wait_ge(saved, NST * b + n + 1)
                s = st[n % XBUF][:, :, 1:]
                nc.gpsimd.tensor_tensor(s, s, bc[n // 2 % 2][:, 1, n % 2:n % 2 + 1, :].broadcast_to([P, ET, L]),
                                        ALU.mult).then_inc(scaled, 1)

            pool.memset(neghalf[:], -0.5).then_inc(consts_made, 1)
            pool.memset(epsilon[:], EPS).then_inc(consts_made, 1)
            pool.memset(ident[:], 0.0).then_inc(consts_made, 1)
            pool.wait_ge(consts_made, 3)
            pool.affine_select(out=ident[:], in_=ident[:], compare_op=ALU.not_equal, fill=1.0, base=0,
                               pattern=[[-1, P]], channel_multiplier=1).then_inc(consts_made, 1)
            pool.wait_ge(small_loaded, 16 * 8)
            rstd_z(0)

            def unit(b, h, inside):
                u = HALVES * b + h
                for jp in range(SLOTS):
                    scans, prepares, ffn = parts(u, inside, jp)
                    if jp == 0 and (inside or 0 < u <= UNITS):
                        rstd_y(u - 1)
                    if scans:
                        scale(u, h, b, 2 * jp)
                    if scans:
                        scale(u, h, b, 2 * jp + 1)
                    if prepares and jp == 2 and h == 1:
                        rstd_z(b + 1)
            schedule(pool, unit)

        @block.vector
        def _(dve):
            def stats_z(b):
                dve.wait_ge(xch_loaded, 16 * (b + 1))
                wait(dve, znb_ready, b)
                for et in range(ET):
                    i = nc.vector.bn_stats(zst[:, et, :], xch[:, et, :])
                i.then_inc(stats_step, 1)
                dve.wait_ge(stats_step, 2 * b + 1)
                nc.vector.memset(waiter[:], 0.0)
                for et in range(ET):
                    i = nc.vector.bn_aggr(zmv[:, et, :], zst[:, et, :])
                i.then_inc(stats_step, 1)

            def shift_z(b):
                dve.wait_ge(rstd_step, 2 * (b + 1))
                nc.vector.scalar_tensor_tensor(znb[:], zmv[:, :, 0], -1.0, zr[:], ALU.mult, ALU.mult).then_inc(znb_ready, 1)

            def convolve(u, taps):
                for tap in taps:
                    if tap == 1:
                        dve.wait_ge(conv_started, u + 1)
                    else:
                        dve.wait_ge(conv_step, (TAPS - 1) * u + tap - 1)
                    for et in range(ET):
                        i = nc.vector.scalar_tensor_tensor(u2[:, et, :], xin[:, et, tap:tap + L], cw[:, et, tap:tap + 1],
                                                           u2[:, et, :], ALU.mult, ALU.add)
                    i.then_inc(conv_step, 1)

            def silu_u(u):
                dve.wait_ge(uth_ready, u + 1)
                nc.vector.scalar_tensor_tensor(u2[:], tmp[:], 1.0, u2[:], ALU.add, ALU.mult).then_inc(u_ready, 1)

            def silu_z(u, h):
                dve.wait_ge(zth_ready, u + 1)
                wait(dve, xht_done, 2 * (u - 1))
                nc.vector.scalar_tensor_tensor(gate[h][:], tmp[:], 1.0, zs[:], ALU.add, ALU.mult).then_inc(zgate_ready, 1)

            def step_u(u, h):
                dve.wait_ge(soft_step, 2 * (u + 1))
                nc.vector.tensor_tensor(delta[h][:], delta[h][:], tmp[:], ALU.add).then_inc(delta_ready, 1)
                dve.wait_ge(delta_ready, u + 1)
                nc.vector.scalar_tensor_tensor(du[h][:], delta[h][:], 0.5, u2[:], ALU.mult, ALU.mult).then_inc(du_ready, 1)

            def feed_state(u, h, n):
                s = st[n % XBUF]
                wait(dve, added, NST * u + n - XBUF + 1)
                if h == 0:
                    nc.vector.memset(s[:, :, 0], 0.0).then_inc(seeded, 1)
                else:
                    nc.vector.tensor_copy(s[:, :, 0], carry[:, n, :]).then_inc(seeded, 1)
                if n == 0:
                    dve.wait_ge(du_ready, u + 1)
                if n % 2 == 0:
                    dve.wait_ge(bc_loaded[n // 2 % 2], 16 * (SLOTS // 2 * u + n // 4 + 1))
                nc.vector.tensor_tensor(s[:, :, 1:], du[h][:],
                                        bc[n // 2 % 2][:, 0, n % 2:n % 2 + 1, :].broadcast_to([P, ET, L]),
                                        ALU.mult).then_inc(input_ready, 1)

            def scan(u, h, b, n):
                s = st[n % XBUF]
                flat = s[:].rearrange("p e t -> p (e t)")
                dve.wait_ge(decays_ready, NST * u + n + 1)
                dve.wait_ge(seeded, NST * u + n + 1)
                dve.wait_ge(input_ready, NST * u + n + 1)
                nc.vector.tensor_tensor_scan(flat, da[n % 2][:].rearrange("p e t -> p (e t)"), flat, 0.0,
                                             ALU.mult, ALU.add).then_inc(scanned, 1)
                if h == 0:
                    dve.wait_ge(scanned, NST * u + n + 1)
                    nc.vector.tensor_copy(carry[:, n, :], s[:, :, L]).then_inc(saved, 1)

            def add(u, h, n):
                if n == 0:
                    dve.wait_ge(acc_started, u + 1)
                dve.wait_ge(scaled, NST * u + n + 1)
                wait(dve, added, NST * u + n)
                nc.vector.tensor_tensor(acc[h][:], acc[h][:], st[n % XBUF][:, :, 1:], ALU.add).then_inc(added, 1)

            def gate_y(u, h):
                dve.wait_ge(added, NST * (u + 1))
                dve.wait_ge(zgate_ready, u + 1)
                nc.vector.scalar_tensor_tensor(gate[h][:], acc[h][:], 0.5, gate[h][:], ALU.mult, ALU.mult).then_inc(yg_ready, 1)

            def add_y(u, h):
                dve.wait_ge(x2_loaded, 16 * (u + 1))
                for t in range(TT):
                    dve.wait_ge(yt_done, 2 * u + t + 1)
                    nc.vector.tensor_tensor(x2[h][:, t, :], ps_misc[t][:], x2[h][:, t, :], ALU.add).then_inc(x2_ready, 1)
                for t in range(TT):
                    dve.wait_ge(x2_ready, 2 * u + t + 1)
                    i = nc.vector.bn_stats(yst[:, t, :], x2[h][:, t, :])
                i.then_inc(ystats_step, 1)
                dve.wait_ge(ystats_step, 2 * u + 1)
                wait(dve, ynb_ready, u)
                nc.vector.memset(waiter[:], 0.0)
                for t in range(TT):
                    i = nc.vector.bn_aggr(ymv[:, t, :], yst[:, t, :])
                i.then_inc(ystats_step, 1)

            def shift_y(u):
                dve.wait_ge(yrstd_step, 2 * (u + 1))
                nc.vector.scalar_tensor_tensor(ynb[:], ymv[:, :, 0], -1.0, yr[:], ALU.mult, ALU.mult).then_inc(ynb_ready, 1)

            def swiglu(w, q):
                p = SLOTS * w + q
                dve.wait_ge(tanh_ready, p + 1)
                nc.vector.scalar_tensor_tensor(th[q % 2][:], th[q % 2][:], 1.0, ps_gate[q % 2][:], ALU.add, ALU.mult
                                               ).then_inc(silu_ready, 1)
                dve.wait_ge(silu_ready, p + 1)
                dve.wait_ge(up_done, p + 1)
                wait(dve, down_done, p - 1)
                nc.vector.tensor_tensor(gu[q % 2][:], th[q % 2][:], ps_up[q % 2][:], ALU.mult).then_inc(gu_ready, 1)

            def finish(w, h):
                dve.wait_ge(down_done, SLOTS * (w + 1))
                for t in range(TT):
                    nc.vector.scalar_tensor_tensor(x2[h][:, t, :], ps_down[t][:], 0.5, x2[h][:, t, :], ALU.mult, ALU.add
                                                   ).then_inc(out_ready, 1)

            nc.vector.memset(nohead[:], 0.0).then_inc(zeros_made, 1)
            for buffer in da:
                nc.vector.memset(buffer[:, :, 0], 0.0).then_inc(zeros_made, 1)
            stats_z(0)
            shift_z(0)
            dve.wait_ge(small_loaded, 16 * 8)
            convolve(0, range(1, TAPS))
            silu_u(0)
            silu_z(0, 0)
            step_u(0, 0)
            feed_state(0, 0, 0)

            def unit(b, h, inside):
                u = HALVES * b + h
                for jp in range(SLOTS):
                    scans, prepares, ffn = parts(u, inside, jp)
                    for n in (2 * jp, 2 * jp + 1):
                        if scans:
                            if n < NST - 1:
                                feed_state(u, h, n + 1)
                            scan(u, h, b, n)
                            if n >= 2:
                                add(u, h, n - 2)
                        if n == 0 and (inside or 0 < u <= UNITS):
                            add_y(u - 1, 1 - h)
                        if n == 1 and (inside or 0 < u <= UNITS):
                            shift_y(u - 1)
                        if prepares and n == 6:
                            convolve(u + 1, [1])
                        if prepares and n == 7:
                            convolve(u + 1, [2, 3])
                        if prepares and n == 8:
                            silu_u(u + 1)
                    if prepares and h == 1:
                        if jp == 1:
                            stats_z(b + 1)
                        if jp == 2:
                            shift_z(b + 1)
                    if ffn:
                        swiglu(*ffn)
                        if ffn[1] == 0 and (inside or u >= 2):
                            finish(u - 2, h)
                    if prepares:
                        if jp == 4:
                            silu_z(u + 1, 1 - h)
                        if jp == 6:
                            step_u(u + 1, 1 - h)
                if scans:
                    add(u, h, NST - 2)
                    if prepares:
                        feed_state(u + 1, 1 - h, 0)
                    add(u, h, NST - 1)
                    gate_y(u, h)
            schedule(dve, unit)
            finish(UNITS - 1, (UNITS - 1) % 2)


def program(nc, shapes):
    ins = [nc.dram_tensor(f"in_{name}", shape, F32, kind="ExternalInput").ap() for name, shape in shapes]
    out = nc.dram_tensor("out_0", (BATCH, SEQ, DIM), F32, kind="ExternalOutput").ap()
    build(nc, *ins, out)


def kernel(x, ctx_1024, L0_xattn_in_proj_w, L0_xattn_conv_w, L0_xattn_conv_b, L0_xattn_x_proj_w, L0_xattn_dt_proj_w,
           L0_xattn_dt_proj_b, L0_xattn_A_log, L0_xattn_D, L0_ffn_w_gate, L0_ffn_w_up, L0_ffn_w_down):
    import concourse.bacc as bacc
    from concourse.bass_utils import run_bass_kernel_spmd

    def tiled(a):
        a = np.asarray(a)
        return a.reshape(-1, P, *a.shape[1:]).swapaxes(0, 1)

    ctx = np.asarray(ctx_1024).reshape(UNITS, L, CT, P).transpose(0, 3, 2, 1)
    arrays = {
        "ctx": ctx,
        "x": np.asarray(x),
        "w_in": tiled(np.asarray(L0_xattn_in_proj_w).T),
        "conv_w": tiled(L0_xattn_conv_w),
        "conv_b": tiled(L0_xattn_conv_b),
        "w_x": tiled(np.asarray(L0_xattn_x_proj_w).T),
        "w_dt": np.asarray(L0_xattn_dt_proj_w).T,
        "dt_b": tiled(L0_xattn_dt_proj_b),
        "a_log": tiled(L0_xattn_A_log),
        "d_skip": tiled(L0_xattn_D),
        "w_gate": tiled(np.asarray(L0_ffn_w_gate).T),
        "w_up": tiled(np.asarray(L0_ffn_w_up).T),
        "w_down": tiled(np.asarray(L0_ffn_w_down).T),
    }
    arrays = {name: np.ascontiguousarray(a) for name, a in arrays.items()}
    nc = bacc.Bacc("TRN2", target_bir_lowering=False, num_devices=1, dynamic_dma_scratch_size=2048)
    program(nc, [(name, a.shape) for name, a in arrays.items()])
    r = run_bass_kernel_spmd(nc, [{f"in_{name}": a for name, a in arrays.items()}], core_ids=[0])
    return np.asarray(r.results[0]["out_0"])
```

```python
from contextlib import ExitStack

import numpy as np
import concourse.bass as bass
from concourse import mybir

P = 128
BATCH, SEQ, DIM = 4, 512, 512
CTX = 256
CHAN = 512
NST = 16
TAPS = 4
RANK = 16
HID = 2048
EPS = 1e-5

L = 256
HALVES = SEQ // L
UNITS = BATCH * HALVES
ET = CHAN // P
CT = CTX // P
DT = DIM // P
TT = L // P
HT = HID // P
SLOTS = 8
LAG = 4
XBUF = 4
GU = 2 * DT * P
EARLY = 8
RING = 6

F32 = mybir.dt.float32
F32R = mybir.dt.float32r
ALU = mybir.AluOpType
ACT = mybir.ActivationFunctionType


def wait(eng, sem, count):
    if not isinstance(count, int) or count > 0:
        eng.wait_ge(sem, count)


def build(nc, ctx_t, x, w_in, conv_w, conv_b, w_x, w_dt, dt_b, a_log, d_skip, w_gu, w_down, out):
    x_chan = x.rearrange("b (e p) t -> b p e t", p=P)
    x_tok = x.rearrange("b (h t p) d -> (b h) p t d", p=P, t=TT)
    out_tok = out.rearrange("b (h t p) d -> (b h) p t d", p=P, t=TT)
    low_parts = nc.dram_tensor("low_parts", (HT, P, GU), F32, kind="Internal").ap()
    bc_rows = nc.dram_tensor("bc_rows", (UNITS, 2, NST, L), F32, kind="Internal").ap()

    with ExitStack() as stack:
        def sb(name, shape, dtype=F32):
            return stack.enter_context(nc.sbuf_tensor(name, shape, dtype))

        def sem(name):
            return stack.enter_context(nc.semaphore(name))

        whigh = sb("whigh", [P, HT, GU], F32R)
        wlow = [sb(f"wlow{i}", [P, GU], F32R) for i in range(2)]
        wd = sb("wd", [P, HID // P, DIM])
        win = sb("win", [P, CT, CHAN])
        wx = sb("wx", [P, ET, RANK + 2 * NST])
        wdt = sb("wdt", [RANK, CHAN])
        cw = sb("cw", [P, ET, TAPS])
        cb = sb("cb", [P, ET])
        dtb = sb("dtb", [P, ET])
        decay = sb("decay", [P, ET, NST])
        dhalf = sb("dhalf", [P, ET])
        ident = sb("ident", [P, P])
        neghalf = sb("neghalf", [P, ET])
        epsilon = sb("epsilon", [P, ET])

        ctxs = sb("ctxs", [P, CT, L])
        xch = sb("xch", [P, ET, DIM])
        xin = sb("xin", [P, ET, TAPS - 1 + L])
        nohead = sb("nohead", [P, ET, TAPS - 1])
        u2 = sb("u2", [P, ET, L])
        tmp = sb("tmp", [P, ET, L])
        zs = sb("zs", [P, ET, L])
        xdbl = sb("xdbl", [RANK + 2 * NST, L])
        delta = [sb(f"delta{h}", [P, ET, L]) for h in range(2)]
        du = [sb(f"du{h}", [P, ET, L]) for h in range(2)]
        gate = [sb(f"gate{h}", [P, ET, L]) for h in range(2)]
        acc = [sb(f"acc{h}", [P, ET, L]) for h in range(2)]
        x2 = [sb(f"x2{h}", [P, TT, DIM]) for h in range(2)]
        st = [sb(f"st{i}", [P, ET, L]) for i in range(XBUF)]
        pair = sb("pair", [P, ET, L])
        carry = sb("carry", [P, ET, NST])
        first = sb("first", [P, ET, NST])
        passed = sb("passed", [P, ET, NST])
        bc = [sb(f"bc{i}", [P, 2, 2, L]) for i in range(2)]
        xhigh = sb("xhigh", [P, DT, L], F32R)
        xlow = sb("xlow", [P, DT, L], F32R)
        gu = [sb(f"gu{i}", [P, L]) for i in range(4)]
        raw = [buf[:].rearrange("p t d -> p (t d)") for buf in (x2[0], x2[1], gate[1], acc[1], delta[1], du[1])]
        waiter = sb("waiter", [P, 1])
        zst = sb("zst", [P, ET, 6])
        zmv = sb("zmv", [P, ET, 2])
        zr = sb("zr", [P, ET])
        znb = sb("znb", [P, ET])
        yst = sb("yst", [P, TT, 6])
        ymv = sb("ymv", [P, TT, 2])
        yr = sb("yr", [P, TT])
        ynb = sb("ynb", [P, TT])

        ps_gu = [stack.enter_context(nc.psum_tensor(f"ps_gu{i}", [P, 2 * L], F32)) for i in range(2)]
        ps_da = [stack.enter_context(nc.psum_tensor(f"ps_da{i}", [P, 2, L], F32)) for i in range(2)]
        ps_down = [stack.enter_context(nc.psum_tensor(f"ps_down{i}", [P, DIM], F32)) for i in range(TT)]
        ps_misc = [stack.enter_context(nc.psum_tensor(f"ps_misc{i}", [P, 2 * L], F32)) for i in range(2)]

        small_loaded = sem("small_loaded")
        raw_loaded = [sem(f"raw_loaded{i}") for i in range(RING)]
        high_made = sem("high_made")
        low_made = sem("low_made")
        late_low_made = sem("late_low_made")
        low_stored = [sem(f"low_stored{i}") for i in range(RING)]
        wlow_loaded = [sem(f"wlow_loaded{i}") for i in range(2)]
        wd_loaded = sem("wd_loaded")
        ctx_loaded = sem("ctx_loaded")
        xch_loaded = sem("xch_loaded")
        x2_loaded = [sem(f"x2_loaded{h}") for h in range(2)]
        rows_stored = sem("rows_stored")
        bc_loaded = [sem(f"bc_loaded{i}") for i in range(2)]
        out_stored = sem("out_stored")
        consts_made = sem("consts_made")
        decay_made = sem("decay_made")
        zeros_made = sem("zeros_made")
        proj_done = sem("proj_done")
        xdbl_done = sem("xdbl_done")
        dt_done = sem("dt_done")
        yt_done = sem("yt_done")
        xht_done = sem("xht_done")
        gateup_done = sem("gateup_done")
        down_done = sem("down_done")
        xin_ready = sem("xin_ready")
        head_ready = sem("head_ready")
        uth_ready = sem("uth_ready")
        xdbl_ready = sem("xdbl_ready")
        dt_read = sem("dt_read")
        soft_step = sem("soft_step")
        z_ready = sem("z_ready")
        zth_ready = sem("zth_ready")
        acc_started = sem("acc_started")
        decays_ready = sem("decays_ready")
        first_ready = sem("first_ready")
        xh_ready = sem("xh_ready")
        xht_ready = sem("xht_ready")
        tanh_ready = sem("tanh_ready")
        conv_started = sem("conv_started")
        conv_step = sem("conv_step")
        rstd_step = sem("rstd_step")
        yrstd_step = sem("yrstd_step")
        scaled = sem("scaled")
        paired = sem("paired")
        u_ready = sem("u_ready")
        delta_ready = sem("delta_ready")
        du_ready = sem("du_ready")
        stats_step = sem("stats_step")
        znb_ready = sem("znb_ready")
        zgate_ready = sem("zgate_ready")
        first_made = sem("first_made")
        passed_on = sem("passed_on")
        input_ready = sem("input_ready")
        seeded = sem("seeded")
        scanned = sem("scanned")
        saved = sem("saved")
        added = sem("added")
        yg_ready = sem("yg_ready")
        x2_ready = sem("x2_ready")
        ystats_step = sem("ystats_step")
        ynb_ready = sem("ynb_ready")
        xlow_ready = sem("xlow_ready")
        silu_ready = sem("silu_ready")
        gu_ready = sem("gu_ready")
        out_ready = sem("out_ready")

        block = stack.enter_context(nc.Block())

        def splits(i):
            return len(range(i, HT, RING))

        def schedule(eng, unit):
            unit(0, 0, False)
            unit(0, 1, False)
            unit(1, 0, False)
            with eng.Fori(0, BATCH - 2) as i:
                unit(i + 1, 1, True)
                unit(i + 2, 0, True)
            unit(BATCH - 1, 1, False)
            unit(BATCH, 0, False)
            unit(BATCH, 1, False)

        def parts(u, inside, jp):
            scans = inside or u < UNITS
            prepares = inside or u < UNITS - 1
            w, q = (u - 1, jp - LAG) if jp >= LAG else (u - 2, SLOTS - LAG + jp)
            feeds = inside or 0 <= w < UNITS
            return scans, prepares, (w, q) if feeds else None

        @block.sync
        def _(sp):
            def load_ctx(u):
                wait(sp, proj_done, 2 * u)
                sp.dma_start(ctxs[:], ctx_t[bass.ds(u, 1)].rearrange("o p c t -> (o p) c t")).then_inc(ctx_loaded, 16)

            def load_xch(b):
                wait(sp, z_ready, HALVES * b)
                sp.dma_start(xch[:], x_chan[bass.ds(b, 1)].rearrange("o p e t -> (o p) e t")).then_inc(xch_loaded, 16)

            def load_x2(u, h):
                if isinstance(u, int) and u < 2:
                    sp.wait_ge(low_stored[h], 16 * splits(h))
                wait(sp, out_stored, 16 * (u - 1))
                sp.dma_start(x2[h][:], x_tok[bass.ds(u, 1)].rearrange("o p t d -> (o p) t d")).then_inc(x2_loaded[h], 16)

            def load_bc(u, jp):
                if jp == 0:
                    sp.wait_ge(rows_stored, 16 * (u + 1))
                wait(sp, input_ready, NST * u + 2 * (jp - 1))
                wait(sp, scaled, NST * u + 2 * (jp - 1))
                src = bc_rows[bass.ds(u, 1), :, 2 * jp:2 * jp + 2, :].rearrange("o a n t -> o a (n t)")
                sp.dma_start(bc[jp % 2][:].rearrange("p a n t -> p a (n t)"),
                             src.broadcast_to([P, 2, 2 * L])).then_inc(bc_loaded[jp % 2], 16)

            def store_rows(u):
                sp.wait_ge(xdbl_ready, u + 1)
                sp.dma_start(bc_rows[bass.ds(u, 1)].rearrange("o a n t -> (o a n) t"),
                             xdbl[RANK:, :]).then_inc(rows_stored, 16)

            def store_out(w, h):
                sp.wait_ge(out_ready, 2 * (w + 1))
                sp.dma_start(out_tok[bass.ds(w, 1)].rearrange("o p t d -> (o p) t d"), x2[h][:]).then_inc(out_stored, 16)

            def load_raw(tile):
                wait(sp, low_stored[tile % RING], 16 * (tile // RING))
                sp.dma_start(raw[tile % RING], w_gu[tile]).then_inc(raw_loaded[tile % RING], 16)

            def store_low(tile):
                if tile < EARLY:
                    sp.wait_ge(low_made, tile + 1)
                else:
                    sp.wait_ge(late_low_made, tile - EARLY + 1)
                sp.dma_start(low_parts[tile], raw[tile % RING]).then_inc(low_stored[tile % RING], 16)

            load_ctx(0)
            for dst, src in ((win, w_in), (cw, conv_w), (cb, conv_b), (dtb, dt_b), (decay, a_log), (dhalf, d_skip),
                             (wx, w_x), (wdt, w_dt)):
                sp.dma_start(dst[:], src).then_inc(small_loaded, 16)
            load_xch(0)
            for tile in range(RING):
                load_raw(tile)
            for tile in range(4):
                store_low(tile)
                load_raw(RING + tile)
            store_rows(0)
            load_bc(0, 0)
            for tile in range(4, EARLY):
                store_low(tile)
            load_raw(RING + 4)
            load_raw(RING + 5)

            def unit(b, h, inside):
                u = HALVES * b + h
                for jp in range(SLOTS):
                    scans, prepares, ffn = parts(u, inside, jp)
                    if prepares and jp == 0:
                        load_ctx(u + 1)
                        if h == 1:
                            load_xch(b + 1)
                    if scans and jp == 0:
                        load_bc(u, 1)
                    if scans and jp < SLOTS - 2:
                        load_bc(u, jp + 2)
                    if not inside and u == 0:
                        for tile in range(2 * RING + 2 * jp, min(2 * RING + 2 * jp + 2, HT)):
                            load_raw(tile)
                        for tile in range(EARLY + 2 * jp, min(EARLY + 2 * jp + 2, HT)):
                            store_low(tile)
                        if jp >= SLOTS // 2:
                            some = slice((2 * jp - SLOTS) * HT // SLOTS, (2 * jp - SLOTS + 2) * HT // SLOTS)
                            sp.dma_start(wd[:, some, :], w_down[:, some, :]).then_inc(wd_loaded, 16)
                        if jp == SLOTS - 1:
                            load_x2(0, 0)
                            load_x2(1, 1)
                            for i in range(RING):
                                sp.wait_ge(low_stored[i], 16 * splits(i))
                            for i in range(2):
                                sp.dma_start(wlow[i][:].bitcast(F32), low_parts[i]).then_inc(wlow_loaded[i], 16)
                    if ffn and ffn[1] == 2:
                        if inside or u >= 2:
                            store_out(u - 2, h)
                        if scans and (inside or u >= 2):
                            load_x2(u, h)
                    if prepares and jp == 5:
                        store_rows(u + 1)
                    if prepares and jp == SLOTS - 2:
                        load_bc(u + 1, 0)
            schedule(sp, unit)
            store_out(UNITS - 1, (UNITS - 1) % 2)
            sp.wait_ge(rows_stored, 16 * UNITS)
            sp.wait_ge(out_stored, 16 * UNITS)

        @block.tensor
        def _(pe):
            def project_in(u, i):
                pe.wait_ge(ctx_loaded, 16 * (u + 1))
                wait(pe, dt_read, 2 * u)
                for e in range(2):
                    et = 2 * i + e
                    for c in range(CT):
                        mm = nc.tensor.matmul(ps_misc[i][:, e * L:(e + 1) * L], win[:, c, et * P:(et + 1) * P],
                                              ctxs[:, c, :], start=(c == 0), stop=(c == CT - 1))
                mm.then_inc(proj_done, 1)

            def project_x(u):
                pe.wait_ge(u_ready, u + 1)
                pe.wait_ge(xin_ready, 2 * (u + 1))
                wait(pe, xlow_ready, 2 * (u - 1))
                for et in range(ET):
                    mm = nc.tensor.matmul(ps_misc[0][0:RANK + 2 * NST, 0:L], wx[:, et, :], u2[:, et, :],
                                          start=(et == 0), stop=(et == ET - 1))
                mm.then_inc(xdbl_done, 1)

            def project_dt(u):
                pe.wait_ge(xdbl_ready, u + 1)
                for et in range(ET):
                    mm = nc.tensor.matmul(ps_misc[1 - et // 2][:, (et % 2) * L:(et % 2 + 1) * L],
                                          wdt[:, et * P:(et + 1) * P], xdbl[0:RANK, :], start=True, stop=True)
                    if et % 2 == 1:
                        mm.then_inc(dt_done, 1)

            def transpose_y(u, h):
                pe.wait_ge(yg_ready, u + 1)
                pe.wait_ge(xin_ready, min(2 * (u + 3), 2 * UNITS) if isinstance(u, int) else 2 * (u + 3))
                for t in range(TT):
                    for et in range(ET):
                        mm = nc.tensor.transpose(ps_misc[t][:, et * P:(et + 1) * P], gate[h][:, et, t * P:(t + 1) * P],
                                                 ident[:])
                    mm.then_inc(yt_done, 1)

            def transpose_norm(u, h):
                rows = gate[h][:].rearrange("p e t -> p (e t)").rearrange("p (t d) -> p t d", t=TT)
                for t in range(TT):
                    pe.wait_ge(xh_ready, 2 * u + t + 1)
                    for k in range(DT):
                        mm = nc.tensor.transpose(ps_misc[t][:, k * P:(k + 1) * P], rows[:, t, k * P:(k + 1) * P],
                                                 ident[:])
                    mm.then_inc(xht_done, 1)

            def down(w, tile):
                g = HT * w + tile
                pe.wait_ge(gu_ready, g + 1)
                if tile == 0:
                    wait(pe, out_ready, 2 * w)
                for t in range(TT):
                    mm = nc.tensor.matmul(ps_down[t][:], gu[tile % 4][:, t * P:(t + 1) * P], wd[:, tile, :],
                                          start=(tile == 0), stop=(tile == HT - 1))
                mm.then_inc(down_done, 1)

            def feed(w, tile, begins):
                g = HT * w + tile
                if tile == 0:
                    pe.wait_ge(xlow_ready, 2 * (w + 1))
                wait(pe, gu_ready, g - 1)
                pe.wait_ge(wlow_loaded[tile % 2], 16 * (HT // 2 * w + tile // 2 + 1))
                for i in range(2):
                    for k in range(DT):
                        cols = slice((i * DT + k) * P, (i * DT + k + 1) * P)
                        products = ((whigh[:, tile, cols], xhigh), (whigh[:, tile, cols], xlow),
                                    (wlow[tile % 2][:, cols], xhigh))
                        for m, (weights, rows) in enumerate(products):
                            mm = nc.tensor.matmul(ps_gu[tile % 2][:, i * L:(i + 1) * L], weights, rows[:, k, :],
                                                  start=(k == 0 and m == 0), stop=(k == DT - 1 and m == 2))
                mm.then_inc(gateup_done, 1)
                if tile >= 2:
                    down(w, tile - 2)
                elif not begins:
                    down(w - 1, HT - 2 + tile)

            pe.wait_ge(small_loaded, 16 * 8)
            project_in(0, 0)
            project_in(0, 1)
            project_x(0)
            project_dt(0)
            pe.wait_ge(consts_made, 4)

            def unit(b, h, inside):
                u = HALVES * b + h
                for jp in range(SLOTS):
                    scans, prepares, ffn = parts(u, inside, jp)
                    follows = inside or 0 < u <= UNITS
                    for n in (2 * jp, 2 * jp + 1):
                        if ffn:
                            w, tile = ffn[0], 2 * ffn[1] + n % 2
                            begins = not inside and w == 0
                            if begins and tile == 0:
                                pe.wait_ge(high_made, HT)
                                pe.wait_ge(wd_loaded, 16 * SLOTS // 2)
                            feed(w, tile, begins)
                        if prepares and n == 1:
                            project_in(u + 1, 0)
                            project_in(u + 1, 1)
                        if follows and n == 2:
                            transpose_y(u - 1, 1 - h)
                        if follows and n == 2 * LAG - 2:
                            transpose_norm(u - 1, 1 - h)
                        if prepares and n == 9:
                            project_x(u + 1)
                        if prepares and n == 10:
                            project_dt(u + 1)
            schedule(pe, unit)
            down(UNITS - 1, HT - 2)
            down(UNITS - 1, HT - 1)

        @block.scalar
        def _(act):
            def take_in(u, h):
                wait(act, conv_step, (TAPS - 1) * u)
                nc.scalar.activation(xin[:, :, 0:TAPS - 1], xin[:, :, L:L + TAPS - 1] if h else nohead[:],
                                     ACT.Copy).then_inc(head_ready, 1)
                act.wait_ge(head_ready, u + 1)
                for i in range(2):
                    act.wait_ge(proj_done, 2 * u + i + 1)
                    nc.scalar.activation(xin[:, 2 * i:2 * i + 2, TAPS - 1:],
                                         ps_misc[i][:].rearrange("p (e t) -> p e t", e=2), ACT.Copy).then_inc(xin_ready, 1)

            def start_conv(u):
                act.wait_ge(xin_ready, 2 * (u + 1))
                wait(act, xdbl_done, u)
                wait(act, du_ready, u)
                wait(act, acc_started, u)
                for et in range(ET):
                    a = nc.scalar.activation(u2[:, et, :], xin[:, et, 0:L], ACT.Identity, scale=cw[:, et, 0:1],
                                             bias=cb[:, et:et + 1])
                a.then_inc(conv_started, 1)

            def tanh_u(u):
                act.wait_ge(conv_step, (TAPS - 1) * (u + 1))
                wait(act, delta_ready, u)
                nc.scalar.activation(tmp[:], u2[:], ACT.Tanh, scale=0.5).then_inc(uth_ready, 1)

            def norm_z(u, h, b):
                act.wait_ge(znb_ready, b + 1)
                wait(act, zgate_ready, u)
                for et in range(ET):
                    a = nc.scalar.activation(zs[:, et, :], xch[:, et, h * L:(h + 1) * L], ACT.Identity,
                                             scale=zr[:, et:et + 1], bias=znb[:, et:et + 1])
                a.then_inc(z_ready, 1)

            def tanh_z(u):
                act.wait_ge(z_ready, u + 1)
                act.wait_ge(u_ready, u + 1)
                nc.scalar.activation(tmp[:], zs[:], ACT.Tanh, scale=0.5).then_inc(zth_ready, 1)

            def take_rows(u):
                act.wait_ge(xdbl_done, u + 1)
                wait(act, rows_stored, 16 * u)
                wait(act, dt_done, 2 * u)
                nc.scalar.activation(xdbl[:], ps_misc[0][0:RANK + 2 * NST, 0:L], ACT.Copy, scale=0.5).then_inc(xdbl_ready, 1)

            def soften(u, h, i):
                if i == 0:
                    act.wait_ge(zgate_ready, u + 1)
                    if isinstance(u, int) and u == 1:
                        act.wait_ge(low_stored[4], 16 * splits(4))
                act.wait_ge(dt_done, 2 * u + i + 1)
                for e in range(2):
                    et = 2 * i + e
                    src = ps_misc[1 - i][:, e * L:(e + 1) * L]
                    nc.scalar.activation(delta[h][:, et, :], src, ACT.Relu, bias=dtb[:, et:et + 1])
                    a = nc.scalar.activation(tmp[:, et, :], src, ACT.Abs, bias=dtb[:, et:et + 1])
                a.then_inc(dt_read, 1)

            def soften_more(u):
                act.wait_ge(dt_read, 2 * (u + 1))
                nc.scalar.activation(tmp[:], tmp[:], ACT.Exp, scale=-1.0).then_inc(soft_step, 1)
                act.wait_ge(soft_step, 2 * u + 1)
                nc.scalar.activation(tmp[:], tmp[:], ACT.Ln, bias=1.0).then_inc(soft_step, 1)

            def start_acc(u, h):
                act.wait_ge(u_ready, u + 1)
                wait(act, yg_ready, u - 1)
                if isinstance(u, int) and u == 1:
                    act.wait_ge(low_stored[3], 16 * splits(3))
                for et in range(ET):
                    a = nc.scalar.activation(acc[h][:, et, :], u2[:, et, :], ACT.Copy, scale=dhalf[:, et:et + 1])
                a.then_inc(acc_started, 1)

            def decays(u, h, n):
                if n == 0:
                    act.wait_ge(delta_ready, u + 1)
                for i in range(2):
                    wait(act, scanned, 2 * (NST * u + n - 1) + i + 1)
                    for e in range(2):
                        et = 2 * i + e
                        a = nc.scalar.activation(ps_da[i][:, e, 1:], delta[h][:, et, 1:], ACT.Exp,
                                                 scale=decay[:, et, n:n + 1])
                    a.then_inc(decays_ready, 1)

            def first_decays(b):
                act.wait_ge(first_made, b + 1)
                nc.scalar.activation(first[:], first[:], ACT.Exp).then_inc(first_ready, 1)

            def split_high(tile):
                act.wait_ge(raw_loaded[tile % RING], 16 * (tile // RING + 1))
                nc.scalar.activation(whigh[:, tile, :], raw[tile % RING], ACT.Copy).then_inc(high_made, 1)

            def tanh_gate(w, tile, more):
                g = HT * w + tile
                act.wait_ge(gateup_done, g + 1)
                if more:
                    act.dma_start(wlow[tile % 2][:].bitcast(F32), low_parts[(tile + 2) % HT]).then_inc(wlow_loaded[tile % 2], 16)
                wait(act, down_done, g - 3)
                nc.scalar.activation(gu[tile % 4][:], ps_gu[tile % 2][:, 0:L], ACT.Tanh, scale=0.5).then_inc(tanh_ready, 1)

            def norm_y(u, h):
                act.wait_ge(ynb_ready, u + 1)
                act.wait_ge(yt_done, 2 * (u + 1))
                rows = gate[h][:].rearrange("p e t -> p (e t)").rearrange("p (t d) -> p t d", t=TT)
                for t in range(TT):
                    nc.scalar.activation(rows[:, t, :], x2[h][:, t, :], ACT.Identity, scale=yr[:, t:t + 1],
                                         bias=ynb[:, t:t + 1]).then_inc(xh_ready, 1)

            def take_norm(u):
                wait(act, gateup_done, HT * u)
                for t in range(TT):
                    act.wait_ge(xht_done, 2 * u + t + 1)
                    nc.scalar.activation(xhigh[:, :, t * P:(t + 1) * P],
                                         ps_misc[t][:].rearrange("p (k l) -> p k l", k=DT), ACT.Copy).then_inc(xht_ready, 1)

            act.wait_ge(small_loaded, 16 * 8)
            nc.scalar.activation(decay[:], decay[:], ACT.Exp).then_inc(decay_made, 1)
            act.wait_ge(decay_made, 1)
            nc.scalar.activation(decay[:], decay[:], ACT.Copy, scale=-1.0).then_inc(decay_made, 1)
            nc.scalar.activation(dhalf[:], dhalf[:], ACT.Copy, scale=0.5).then_inc(decay_made, 1)
            act.wait_ge(zeros_made, 3)
            act.wait_ge(decay_made, 3)
            take_in(0, 0)
            start_conv(0)
            split_high(0)
            tanh_u(0)
            norm_z(0, 0, 0)
            tanh_z(0)
            split_high(1)
            take_rows(0)
            split_high(2)
            split_high(3)
            soften(0, 0, 0)
            soften(0, 0, 1)
            soften_more(0)
            start_acc(0, 0)
            decays(0, 0, 0)
            for tile in range(4, EARLY):
                split_high(tile)

            def unit(b, h, inside):
                u = HALVES * b + h
                for jp in range(SLOTS):
                    scans, prepares, ffn = parts(u, inside, jp)
                    follows = inside or 0 < u <= UNITS
                    for n in (2 * jp, 2 * jp + 1):
                        if ffn:
                            w, q = ffn
                            tanh_gate(w, 2 * q + n % 2, inside or w < UNITS - 1 or q < SLOTS - 1)
                        if not inside and u == 0 and EARLY + n < HT:
                            split_high(EARLY + n)
                        if prepares and n == 2:
                            take_in(u + 1, 1 - h)
                        if prepares and n == 3:
                            start_conv(u + 1)
                        if follows and n == 2 * LAG - 3:
                            norm_y(u - 1, 1 - h)
                        if follows and n == 2 * LAG - 2:
                            take_norm(u - 1)
                        if prepares and n == 7:
                            tanh_u(u + 1)
                        if prepares and n == 8:
                            norm_z(u + 1, 1 - h, b + h)
                        if prepares and n == 9:
                            tanh_z(u + 1)
                            take_rows(u + 1)
                        if prepares and n == 10:
                            start_acc(u + 1, 1 - h)
                        if prepares and n in (11, 12):
                            soften(u + 1, 1 - h, n - 11)
                        if prepares and n == 13:
                            soften_more(u + 1)
                        if prepares and h == 0 and n == 15:
                            first_decays(b)
                        if scans and n < NST - 1:
                            decays(u, h, n + 1)
                        elif prepares and n == NST - 1:
                            decays(u + 1, 1 - h, 0)
            schedule(act, unit)

        @block.gpsimd
        def _(pool):
            def rstd_z(b):
                pool.wait_ge(stats_step, 2 * (b + 1))
                wait(pool, z_ready, HALVES * b)
                nc.gpsimd.tensor_tensor(zr[:], zmv[:, :, 1], epsilon[:], ALU.add).then_inc(rstd_step, 1)
                pool.wait_ge(rstd_step, 2 * b + 1)
                nc.gpsimd.tensor_tensor(zr[:], zr[:], neghalf[:], ALU.pow).then_inc(rstd_step, 1)

            def rstd_y(u):
                pool.wait_ge(ystats_step, 2 * (u + 1))
                wait(pool, xh_ready, 2 * u)
                nc.gpsimd.tensor_tensor(yr[:], ymv[:, :, 1], epsilon[:, 0:TT], ALU.add).then_inc(yrstd_step, 1)
                pool.wait_ge(yrstd_step, 2 * u + 1)
                nc.gpsimd.tensor_tensor(yr[:], yr[:], neghalf[:, 0:TT], ALU.pow).then_inc(yrstd_step, 1)

            def split_low(tile):
                pool.wait_ge(raw_loaded[tile % RING], 16 * (tile // RING + 1))
                pool.wait_ge(high_made, tile + 1)
                nc.gpsimd.tensor_tensor(raw[tile % RING].bitcast(F32R), raw[tile % RING], whigh[:, tile, :].bitcast(F32),
                                        ALU.subtract).then_inc(low_made, 1)

            def scale(u, h, b, n):
                if n % 2 == 0:
                    pool.wait_ge(bc_loaded[n // 2 % 2], 16 * (SLOTS // 2 * u + n // 4 + 1))
                pool.wait_ge(scanned, 2 * (NST * u + n + 1))
                if h == 0:
                    pool.wait_ge(saved, NST * b + n + 1)
                s = st[n % XBUF]
                nc.gpsimd.tensor_tensor(s[:], s[:], bc[n // 2 % 2][:, 1, n % 2:n % 2 + 1, :].broadcast_to([P, ET, L]),
                                        ALU.mult).then_inc(scaled, 1)

            def add_pair(u, jp):
                pool.wait_ge(scaled, NST * u + 2 * jp + 2)
                wait(pool, added, SLOTS * u + jp)
                nc.gpsimd.tensor_tensor(pair[:], st[2 * jp % XBUF][:], st[(2 * jp + 1) % XBUF][:], ALU.add
                                        ).then_inc(paired, 1)

            pool.memset(neghalf[:], -0.5).then_inc(consts_made, 1)
            pool.memset(epsilon[:], EPS).then_inc(consts_made, 1)
            pool.memset(ident[:], 0.0).then_inc(consts_made, 1)
            pool.wait_ge(consts_made, 3)
            pool.affine_select(out=ident[:], in_=ident[:], compare_op=ALU.not_equal, fill=1.0, base=0,
                               pattern=[[-1, P]], channel_multiplier=1).then_inc(consts_made, 1)
            pool.wait_ge(small_loaded, 16 * 8)
            rstd_z(0)
            for tile in range(EARLY):
                split_low(tile)

            def unit(b, h, inside):
                u = HALVES * b + h
                for jp in range(SLOTS):
                    scans, prepares, ffn = parts(u, inside, jp)
                    if scans:
                        scale(u, h, b, 2 * jp)
                    if prepares and jp == 2 and h == 1:
                        rstd_z(b + 1)
                    if scans:
                        scale(u, h, b, 2 * jp + 1)
                    if jp == 1 and (inside or 0 < u <= UNITS):
                        rstd_y(u - 1)
                    if scans:
                        add_pair(u, jp)
            schedule(pool, unit)

        @block.vector
        def _(dve):
            def stats_z(b):
                dve.wait_ge(xch_loaded, 16 * (b + 1))
                wait(dve, znb_ready, b)
                for et in range(ET):
                    i = nc.vector.bn_stats(zst[:, et, :], xch[:, et, :])
                i.then_inc(stats_step, 1)
                dve.wait_ge(stats_step, 2 * b + 1)
                nc.vector.memset(waiter[:], 0.0)
                for et in range(ET):
                    i = nc.vector.bn_aggr(zmv[:, et, :], zst[:, et, :])
                i.then_inc(stats_step, 1)

            def shift_z(b):
                dve.wait_ge(rstd_step, 2 * (b + 1))
                nc.vector.scalar_tensor_tensor(znb[:], zmv[:, :, 0], -1.0, zr[:], ALU.mult, ALU.mult).then_inc(znb_ready, 1)

            def convolve(u, taps):
                for tap in taps:
                    if tap == 1:
                        dve.wait_ge(conv_started, u + 1)
                    else:
                        dve.wait_ge(conv_step, (TAPS - 1) * u + tap - 1)
                    for et in range(ET):
                        i = nc.vector.scalar_tensor_tensor(u2[:, et, :], xin[:, et, tap:tap + L], cw[:, et, tap:tap + 1],
                                                           u2[:, et, :], ALU.mult, ALU.add)
                    i.then_inc(conv_step, 1)

            def silu_u(u):
                dve.wait_ge(uth_ready, u + 1)
                nc.vector.scalar_tensor_tensor(u2[:], tmp[:], 1.0, u2[:], ALU.add, ALU.mult).then_inc(u_ready, 1)

            def split_low(tile):
                dve.wait_ge(raw_loaded[tile % RING], 16 * (tile // RING + 1))
                dve.wait_ge(high_made, tile + 1)
                nc.vector.tensor_tensor(raw[tile % RING].bitcast(F32R), raw[tile % RING], whigh[:, tile, :].bitcast(F32),
                                        ALU.subtract).then_inc(late_low_made, 1)

            def silu_z(u, h):
                dve.wait_ge(zth_ready, u + 1)
                if isinstance(u, int) and u == 1:
                    dve.wait_ge(low_stored[2], 16 * splits(2))
                wait(dve, xht_done, 2 * (u - 1))
                nc.vector.scalar_tensor_tensor(gate[h][:], tmp[:], 1.0, zs[:], ALU.add, ALU.mult).then_inc(zgate_ready, 1)

            def step_u(u, h):
                dve.wait_ge(soft_step, 2 * (u + 1))
                nc.vector.tensor_tensor(delta[h][:], delta[h][:], tmp[:], ALU.add).then_inc(delta_ready, 1)

            def times_u(u, h):
                dve.wait_ge(delta_ready, u + 1)
                if isinstance(u, int) and u == 1:
                    dve.wait_ge(low_stored[5], 16 * splits(5))
                nc.vector.scalar_tensor_tensor(du[h][:], delta[h][:], 0.5, u2[:], ALU.mult, ALU.mult).then_inc(du_ready, 1)

            def make_first(b):
                for et in range(ET):
                    i = nc.vector.tensor_scalar(first[:, et, :], decay[:, et, :], delta[1][:, et, 0:1], None, ALU.mult)
                i.then_inc(first_made, 1)

            def pass_on(b):
                dve.wait_ge(first_ready, b + 1)
                dve.wait_ge(saved, NST * (b + 1))
                nc.vector.tensor_tensor(passed[:], carry[:], first[:], ALU.mult).then_inc(passed_on, 1)

            def feed_state(u, h, b, n):
                s = st[n % XBUF]
                if n == 0:
                    dve.wait_ge(du_ready, u + 1)
                if n % 2 == 0:
                    dve.wait_ge(bc_loaded[n // 2 % 2], 16 * (SLOTS // 2 * u + n // 4 + 1))
                    wait(dve, paired, SLOTS * u + n // 2 - 1)
                nc.vector.tensor_tensor(s[:], du[h][:], bc[n // 2 % 2][:, 0, n % 2:n % 2 + 1, :].broadcast_to([P, ET, L]),
                                        ALU.mult).then_inc(input_ready, 1)

            def seed(u, b, n):
                s = st[n % XBUF]
                dve.wait_ge(input_ready, NST * u + n + 1)
                dve.wait_ge(passed_on, b + 1)
                nc.vector.tensor_tensor(s[:, :, 0], s[:, :, 0], passed[:, :, n], ALU.add).then_inc(seeded, 1)

            def scan(u, h, b, n):
                dve.wait_ge(input_ready, NST * u + n + 1)
                if h == 1:
                    dve.wait_ge(seeded, NST * b + n + 1)
                for i in range(2):
                    flat = st[n % XBUF][:, 2 * i:2 * i + 2, :].rearrange("p e t -> p (e t)")
                    dve.wait_ge(decays_ready, 2 * (NST * u + n) + i + 1)
                    nc.vector.tensor_tensor_scan(flat, ps_da[i][:].rearrange("p e t -> p (e t)"), flat, 0.0,
                                                 ALU.mult, ALU.add).then_inc(scanned, 1)

            def save(u, b, n):
                dve.wait_ge(scanned, 2 * (NST * u + n + 1))
                nc.vector.tensor_copy(carry[:, :, n], st[n % XBUF][:, :, L - 1]).then_inc(saved, 1)

            def add(u, h, jp):
                if jp == 0:
                    dve.wait_ge(acc_started, u + 1)
                dve.wait_ge(paired, SLOTS * u + jp + 1)
                wait(dve, added, SLOTS * u + jp)
                nc.vector.tensor_tensor(acc[h][:], acc[h][:], pair[:], ALU.add).then_inc(added, 1)

            def gate_y(u, h):
                dve.wait_ge(added, SLOTS * (u + 1))
                dve.wait_ge(zgate_ready, u + 1)
                nc.vector.scalar_tensor_tensor(gate[h][:], acc[h][:], 0.5, gate[h][:], ALU.mult, ALU.mult).then_inc(yg_ready, 1)

            def add_y(u, h, b):
                dve.wait_ge(x2_loaded[h], 16 * (b + 1))
                for t in range(TT):
                    dve.wait_ge(yt_done, 2 * u + t + 1)
                    nc.vector.tensor_tensor(x2[h][:, t, :], ps_misc[t][:], x2[h][:, t, :], ALU.add).then_inc(x2_ready, 1)
                for t in range(TT):
                    dve.wait_ge(x2_ready, 2 * u + t + 1)
                    i = nc.vector.bn_stats(yst[:, t, :], x2[h][:, t, :])
                i.then_inc(ystats_step, 1)
                dve.wait_ge(ystats_step, 2 * u + 1)
                wait(dve, ynb_ready, u)
                nc.vector.memset(waiter[:], 0.0)
                for t in range(TT):
                    i = nc.vector.bn_aggr(ymv[:, t, :], yst[:, t, :])
                i.then_inc(ystats_step, 1)

            def shift_y(u):
                dve.wait_ge(yrstd_step, 2 * (u + 1))
                nc.vector.scalar_tensor_tensor(ynb[:], ymv[:, :, 0], -1.0, yr[:], ALU.mult, ALU.mult).then_inc(ynb_ready, 1)

            def take_low(u):
                for t in range(TT):
                    dve.wait_ge(xht_ready, 2 * u + t + 1)
                    nc.vector.tensor_tensor(xlow[:, :, t * P:(t + 1) * P],
                                            ps_misc[t][:].rearrange("p (k l) -> p k l", k=DT),
                                            xhigh[:, :, t * P:(t + 1) * P].bitcast(F32), ALU.subtract
                                            ).then_inc(xlow_ready, 1)

            def silu_gate(w, tile):
                g = HT * w + tile
                dve.wait_ge(tanh_ready, g + 1)
                nc.vector.scalar_tensor_tensor(gu[tile % 4][:], gu[tile % 4][:], 1.0, ps_gu[tile % 2][:, 0:L],
                                               ALU.add, ALU.mult).then_inc(silu_ready, 1)

            def times_up(w, tile):
                g = HT * w + tile
                dve.wait_ge(silu_ready, g + 1)
                nc.vector.tensor_tensor(gu[tile % 4][:], gu[tile % 4][:], ps_gu[tile % 2][:, L:2 * L], ALU.mult
                                        ).then_inc(gu_ready, 1)

            def finish(w, h):
                dve.wait_ge(down_done, HT * (w + 1))
                for t in range(TT):
                    nc.vector.scalar_tensor_tensor(x2[h][:, t, :], ps_down[t][:], 0.5, x2[h][:, t, :], ALU.mult, ALU.add
                                                   ).then_inc(out_ready, 1)

            nc.vector.memset(nohead[:], 0.0).then_inc(zeros_made, 1)
            for bank in ps_da:
                nc.vector.memset(bank[:, :, 0], 0.0).then_inc(zeros_made, 1)
            stats_z(0)
            shift_z(0)
            dve.wait_ge(small_loaded, 16 * 8)
            convolve(0, range(1, TAPS))
            silu_u(0)
            silu_z(0, 0)
            step_u(0, 0)
            times_u(0, 0)

            def unit(b, h, inside):
                u = HALVES * b + h
                for jp in range(SLOTS):
                    scans, prepares, ffn = parts(u, inside, jp)
                    follows = inside or 0 < u <= UNITS
                    for n in (2 * jp, 2 * jp + 1):
                        if n == 2 * LAG + 2 and (inside or u >= 2) and ffn:
                            finish(u - 2, h)
                        if scans:
                            feed_state(u, h, b, n)
                            if h == 1 and n == 0:
                                pass_on(b)
                        if ffn:
                            w, tile = ffn[0], 2 * ffn[1] + n % 2
                            silu_gate(w, tile)
                        if scans and h == 1:
                            seed(u, b, n)
                        if ffn:
                            times_up(w, tile)
                        if scans:
                            scan(u, h, b, n)
                            if h == 0:
                                save(u, b, n)
                        if follows and n == 1:
                            add(u - 1, 1 - h, SLOTS - 1)
                            gate_y(u - 1, 1 - h)
                        if not inside and u == 0 and EARLY + n < HT:
                            split_low(EARLY + n)
                        if follows and n == 3:
                            add_y(u - 1, 1 - h, b if h else b - 1)
                        if follows and n == 4:
                            shift_y(u - 1)
                        if follows and n == 2 * LAG - 2:
                            take_low(u - 1)
                        if prepares and 4 <= n < 4 + TAPS - 1:
                            convolve(u + 1, [n - 3])
                        if prepares and n == 5 and h == 1:
                            shift_z(b + 1)
                        if prepares and n == 8:
                            silu_u(u + 1)
                        if prepares and n == 10:
                            silu_z(u + 1, 1 - h)
                        if prepares and n == 13:
                            step_u(u + 1, 1 - h)
                        if prepares and n == 14:
                            times_u(u + 1, 1 - h)
                        if prepares and h == 0 and n == 14:
                            make_first(b)
                    if scans and jp > 0:
                        add(u, h, jp - 1)
                    if prepares and h == 1 and jp == 1:
                        stats_z(b + 1)
            schedule(dve, unit)
            finish(UNITS - 1, (UNITS - 1) % 2)


def program(nc, shapes):
    ins = [nc.dram_tensor(f"in_{name}", shape, F32, kind="ExternalInput").ap() for name, shape in shapes]
    out = nc.dram_tensor("out_0", (BATCH, SEQ, DIM), F32, kind="ExternalOutput").ap()
    build(nc, *ins, out)


def kernel(x, ctx_1024, L0_xattn_in_proj_w, L0_xattn_conv_w, L0_xattn_conv_b, L0_xattn_x_proj_w, L0_xattn_dt_proj_w,
           L0_xattn_dt_proj_b, L0_xattn_A_log, L0_xattn_D, L0_ffn_w_gate, L0_ffn_w_up, L0_ffn_w_down):
    import concourse.bacc as bacc
    from concourse.bass_utils import run_bass_kernel_spmd

    def tiled(a):
        a = np.asarray(a)
        return a.reshape(-1, P, *a.shape[1:]).swapaxes(0, 1)

    ctx = np.asarray(ctx_1024).reshape(UNITS, L, CT, P).transpose(0, 3, 2, 1)
    gate_up = np.stack([np.asarray(L0_ffn_w_gate), np.asarray(L0_ffn_w_up)]).reshape(2, HT, P, DT, P)
    arrays = {
        "ctx": ctx,
        "x": np.asarray(x),
        "w_in": tiled(np.asarray(L0_xattn_in_proj_w).T),
        "conv_w": tiled(L0_xattn_conv_w),
        "conv_b": tiled(L0_xattn_conv_b),
        "w_x": tiled(np.asarray(L0_xattn_x_proj_w).T),
        "w_dt": np.asarray(L0_xattn_dt_proj_w).T,
        "dt_b": tiled(L0_xattn_dt_proj_b),
        "a_log": tiled(L0_xattn_A_log),
        "d_skip": tiled(L0_xattn_D),
        "w_gu": gate_up.transpose(1, 4, 0, 3, 2).reshape(HT, P, GU),
        "w_down": tiled(np.asarray(L0_ffn_w_down).T),
    }
    arrays = {name: np.ascontiguousarray(a) for name, a in arrays.items()}
    nc = bacc.Bacc("TRN2", target_bir_lowering=False, num_devices=1, dynamic_dma_scratch_size=2048)
    program(nc, [(name, a.shape) for name, a in arrays.items()])
    r = run_bass_kernel_spmd(nc, [{f"in_{name}": a for name, a in arrays.items()}], core_ids=[0])
    return np.asarray(r.results[0]["out_0"])
```

```python
from contextlib import ExitStack

import numpy as np
import concourse.bass as bass
from concourse import mybir

P = 128
BATCH, SEQ, DIM = 4, 512, 512
CTX = 256
CHAN = 512
NST = 16
TAPS = 4
RANK = 16
HID = 2048
EPS = 1e-5

L = 256
HALVES = SEQ // L
UNITS = BATCH * HALVES
ET = CHAN // P
CT = CTX // P
DT = DIM // P
TT = L // P
HT = HID // P
SLOTS = 8
LAG = 7
XBUF = 4
GU = 2 * DT * P
SPLIT_IN = (0, 1, 2, 3, 4, 5, 6, 7, 0, 1, 4, 5, 0, 1, 6, 7)
RAWS = len(set(SPLIT_IN))
POOL_SPLITS, POOL_LATE_SPLITS = (0, 1, 2, 3, 4, 5), (11, 13, 14, 15)
DVE_SPLITS, DVE_LATE_SPLITS = (6, 7, 8, 9), (10, 12)

F32 = mybir.dt.float32
F32R = mybir.dt.float32r
ALU = mybir.AluOpType
ACT = mybir.ActivationFunctionType


def wait(eng, sem, count):
    if not isinstance(count, int) or count > 0:
        eng.wait_ge(sem, count)


def build(nc, ctx_t, x, w_in, conv_w, conv_b, w_x, w_dt, dt_b, a_log, d_skip, w_gu, w_down, out):
    x_chan = x.rearrange("b (e p) t -> b p e t", p=P)
    x_tok = x.rearrange("b (h t p) d -> (b h) p t d", p=P, t=TT)
    out_tok = out.rearrange("b (h t p) d -> (b h) p t d", p=P, t=TT)
    low_parts = nc.dram_tensor("low_parts", (HT, P, GU), F32, kind="Internal").ap()
    bc_rows = nc.dram_tensor("bc_rows", (UNITS, 2, NST, L), F32, kind="Internal").ap()

    with ExitStack() as stack:
        def sb(name, shape, dtype=F32):
            return stack.enter_context(nc.sbuf_tensor(name, shape, dtype))

        def sem(name):
            return stack.enter_context(nc.semaphore(name))

        whigh = sb("whigh", [P, HT, GU], F32R)
        wlow = [sb(f"wlow{i}", [P, GU], F32R) for i in range(2)]
        wd = sb("wd", [P, HID // P, DIM])
        win = sb("win", [P, CT, CHAN])
        wx = sb("wx", [P, ET, RANK + 2 * NST])
        wdt = sb("wdt", [RANK, CHAN])
        cw = sb("cw", [P, ET, TAPS])
        cb = sb("cb", [P, ET])
        dtb = sb("dtb", [P, ET])
        decay = sb("decay", [P, ET, NST])
        dhalf = sb("dhalf", [P, ET])
        ident = sb("ident", [P, P])
        neghalf = sb("neghalf", [P, ET])
        epsilon = sb("epsilon", [P, ET])

        ctxs = sb("ctxs", [P, CT, L])
        xch = sb("xch", [P, ET, DIM])
        xin = sb("xin", [P, ET, TAPS - 1 + L])
        nohead = sb("nohead", [P, ET, TAPS - 1])
        u2 = sb("u2", [P, ET, L])
        tmp = sb("tmp", [P, ET, L])
        xdbl = sb("xdbl", [RANK + 2 * NST, L])
        delta = [sb(f"delta{h}", [P, ET, L]) for h in range(2)]
        du = [sb(f"du{h}", [P, ET, L]) for h in range(2)]
        gate = [sb(f"gate{h}", [P, ET, L]) for h in range(2)]
        acc = [sb(f"acc{h}", [P, ET, L]) for h in range(2)]
        x2 = [sb(f"x2{h}", [P, TT, DIM]) for h in range(2)]
        st = [sb(f"st{i}", [P, ET, L]) for i in range(XBUF)]
        carry = sb("carry", [P, ET, NST])
        first = sb("first", [P, ET, NST])
        passed = sb("passed", [P, ET, NST])
        bc = [sb(f"bc{i}", [P, 2, 2, L]) for i in range(2)]
        xhigh = [sb(f"xhigh{h}", [P, DT, L], F32R) for h in range(2)]
        xlow = [sb(f"xlow{h}", [P, DT, L], F32R) for h in range(2)]
        gu = [sb(f"gu{i}", [P, L]) for i in range(4)]
        raw = [buf[:].rearrange("p t d -> p (t d)") for buf in (
            x2[0], x2[1], st[2], st[3], gate[1], acc[1], delta[1], du[1])]
        waiter = sb("waiter", [P, 1])
        zst = sb("zst", [P, ET, 6])
        zmv = sb("zmv", [P, ET, 2])
        zr = sb("zr", [P, ET])
        znb = sb("znb", [P, ET])
        yst = sb("yst", [P, TT, 6])
        ymv = sb("ymv", [P, TT, 2])
        yr = sb("yr", [P, TT])
        ynb = sb("ynb", [P, TT])

        ps_gu = [stack.enter_context(nc.psum_tensor(f"ps_gu{i}", [P, 2 * L], F32)) for i in range(2)]
        ps_da = [stack.enter_context(nc.psum_tensor(f"ps_da{i}", [P, 2, L], F32)) for i in range(2)]
        ps_down = [stack.enter_context(nc.psum_tensor(f"ps_down{i}", [P, DIM], F32)) for i in range(TT)]
        ps_misc = [stack.enter_context(nc.psum_tensor(f"ps_misc{i}", [P, 2 * L], F32)) for i in range(2)]

        small_loaded = sem("small_loaded")
        raw_loaded = [sem(f"raw_loaded{i}") for i in range(RAWS)]
        high_made = sem("high_made")
        pool_low_made = sem("pool_low_made")
        dve_low_made = sem("dve_low_made")
        low_stored = [sem(f"low_stored{i}") for i in range(RAWS)]
        wlow_loaded = [sem(f"wlow_loaded{i}") for i in range(2)]
        wd_loaded = sem("wd_loaded")
        ctx_loaded = sem("ctx_loaded")
        xch_loaded = sem("xch_loaded")
        x2_loaded = [sem(f"x2_loaded{h}") for h in range(2)]
        rows_stored = sem("rows_stored")
        bc_loaded = [sem(f"bc_loaded{i}") for i in range(2)]
        out_stored = sem("out_stored")
        consts_made = sem("consts_made")
        decay_made = sem("decay_made")
        zeros_made = sem("zeros_made")
        proj_done = sem("proj_done")
        xdbl_done = sem("xdbl_done")
        dt_done = sem("dt_done")
        yt_done = sem("yt_done")
        xht_done = sem("xht_done")
        gateup_done = sem("gateup_done")
        down_done = sem("down_done")
        xin_ready = sem("xin_ready")
        head_ready = sem("head_ready")
        uth_ready = sem("uth_ready")
        xdbl_ready = sem("xdbl_ready")
        dt_read = sem("dt_read")
        soft_step = sem("soft_step")
        z_ready = sem("z_ready")
        zth_ready = sem("zth_ready")
        acc_started = sem("acc_started")
        decays_ready = sem("decays_ready")
        first_ready = sem("first_ready")
        xh_ready = sem("xh_ready")
        xht_ready = sem("xht_ready")
        tanh_ready = sem("tanh_ready")
        conv_started = sem("conv_started")
        conv_step = sem("conv_step")
        rstd_step = sem("rstd_step")
        yrstd_step = sem("yrstd_step")
        scaled = sem("scaled")
        paired = sem("paired")
        u_ready = sem("u_ready")
        delta_ready = sem("delta_ready")
        du_ready = sem("du_ready")
        stats_step = sem("stats_step")
        znb_ready = sem("znb_ready")
        zgate_ready = sem("zgate_ready")
        first_made = sem("first_made")
        passed_on = sem("passed_on")
        input_ready = sem("input_ready")
        seeded = sem("seeded")
        scanned = sem("scanned")
        saved = sem("saved")
        added = sem("added")
        yg_ready = sem("yg_ready")
        x2_ready = sem("x2_ready")
        ystats_step = sem("ystats_step")
        ynb_ready = sem("ynb_ready")
        xlow_ready = sem("xlow_ready")
        silu_ready = sem("silu_ready")
        gu_ready = sem("gu_ready")
        out_ready = sem("out_ready")

        block = stack.enter_context(nc.Block())

        def splits(i):
            return SPLIT_IN.count(i)

        def turn(tile):
            return SPLIT_IN[:tile].count(SPLIT_IN[tile])

        def schedule(eng, unit):
            unit(0, 0, False)
            unit(0, 1, False)
            unit(1, 0, False)
            with eng.Fori(0, BATCH - 2) as i:
                unit(i + 1, 1, True)
                unit(i + 2, 0, True)
            unit(BATCH - 1, 1, False)
            unit(BATCH, 0, False)
            unit(BATCH, 1, False)

        def feeding(u, inside, n):
            w, tile = (u - 1, n - LAG) if n >= LAG else (u - 2, HT - LAG + n)
            return (w, tile) if inside or 0 <= w < UNITS else None

        @block.sync
        def _(sp):
            def load_ctx(u):
                wait(sp, proj_done, 2 * u)
                sp.dma_start(ctxs[:], ctx_t[bass.ds(u, 1)].rearrange("o p c t -> (o p) c t")).then_inc(ctx_loaded, 16)

            def load_xch(b):
                wait(sp, z_ready, HALVES * b)
                sp.dma_start(xch[:], x_chan[bass.ds(b, 1)].rearrange("o p e t -> (o p) e t")).then_inc(xch_loaded, 16)

            def load_x2(u, h):
                if isinstance(u, int) and u < 2:
                    sp.wait_ge(low_stored[h], 16 * splits(h))
                wait(sp, out_stored, 16 * (u - 1))
                sp.dma_start(x2[h][:], x_tok[bass.ds(u, 1)].rearrange("o p t d -> (o p) t d")).then_inc(x2_loaded[h], 16)

            def load_bc(u, jp):
                if jp == 0:
                    sp.wait_ge(rows_stored, 16 * (u + 1))
                wait(sp, input_ready, NST * u + 2 * (jp - 1))
                wait(sp, scaled, NST * u + 2 * (jp - 1))
                src = bc_rows[bass.ds(u, 1), :, 2 * jp:2 * jp + 2, :].rearrange("o a n t -> o a (n t)")
                sp.dma_start(bc[jp % 2][:].rearrange("p a n t -> p a (n t)"),
                             src.broadcast_to([P, 2, 2 * L])).then_inc(bc_loaded[jp % 2], 16)

            def store_rows(u):
                sp.wait_ge(xdbl_ready, u + 1)
                sp.dma_start(bc_rows[bass.ds(u, 1)].rearrange("o a n t -> (o a n) t"),
                             xdbl[RANK:, :]).then_inc(rows_stored, 16)

            def store_out(w, h):
                sp.wait_ge(out_ready, 2 * (w + 1))
                sp.dma_start(out_tok[bass.ds(w, 1)].rearrange("o p t d -> (o p) t d"), x2[h][:]).then_inc(out_stored, 16)

            def load_raw(tile):
                wait(sp, low_stored[SPLIT_IN[tile]], 16 * turn(tile))
                sp.dma_start(raw[SPLIT_IN[tile]], w_gu[tile]).then_inc(raw_loaded[SPLIT_IN[tile]], 16)

            def store_low(tile):
                if tile in POOL_SPLITS + POOL_LATE_SPLITS:
                    sp.wait_ge(pool_low_made, (POOL_SPLITS + POOL_LATE_SPLITS).index(tile) + 1)
                else:
                    sp.wait_ge(dve_low_made, (DVE_SPLITS + DVE_LATE_SPLITS).index(tile) + 1)
                sp.dma_start(low_parts[tile], raw[SPLIT_IN[tile]]).then_inc(low_stored[SPLIT_IN[tile]], 16)

            load_ctx(0)
            for dst, src in ((win, w_in), (cw, conv_w), (cb, conv_b), (dtb, dt_b), (decay, a_log), (dhalf, d_skip),
                             (wx, w_x), (wdt, w_dt)):
                sp.dma_start(dst[:], src).then_inc(small_loaded, 16)
            load_xch(0)
            for tile in range(RAWS):
                load_raw(tile)
            store_low(0)
            load_ctx(1)
            store_low(1)
            load_raw(8)
            store_low(2)
            load_raw(9)
            store_low(3)
            store_rows(0)
            load_bc(0, 0)
            load_bc(0, 1)
            store_low(4)
            store_low(5)
            load_raw(10)
            store_low(6)
            load_raw(11)
            for tile in (7, 8, 9):
                store_low(tile)
            for tile in (12, 13, 14, 15):
                load_raw(tile)

            def unit(b, h, inside):
                u = HALVES * b + h
                scans, prepares = inside or u < UNITS, inside or u < UNITS - 1
                for jp in range(SLOTS):
                    if jp == 0 and (inside or u > 0):
                        if prepares:
                            load_ctx(u + 1)
                        if scans and h == 0:
                            load_xch(b)
                        if scans:
                            load_bc(u, 0)
                            load_bc(u, 1)
                    if scans and jp < SLOTS - 2:
                        load_bc(u, jp + 2)
                    if not inside and u == 0:
                        for tile in ((10, 11), (12, 13), (14,), (15,), (), (), (), ())[jp]:
                            store_low(tile)
                        if jp == SLOTS // 2:
                            for i in range(RAWS):
                                sp.wait_ge(low_stored[i], 16 * splits(i))
                            for i in range(2):
                                sp.dma_start(wlow[i][:].bitcast(F32), low_parts[i]).then_inc(wlow_loaded[i], 16)
                        if jp == SLOTS - 2:
                            load_x2(0, 0)
                    if not inside and u < HALVES:
                        share = SLOTS * u + jp - 2
                        if 0 <= share < SLOTS:
                            some = slice(share * HT // SLOTS, (share + 1) * HT // SLOTS)
                            sp.dma_start(wd[:, some, :], w_down[:, some, :]).then_inc(wd_loaded, 16)
                        if u == 1 and jp == SLOTS // 2:
                            load_x2(1, 1)
                    if jp == (LAG + 3) // 2 and (inside or 2 <= u <= UNITS):
                        store_out(u - 2, h)
                        if scans:
                            load_x2(u, h)
                    if prepares and jp == 5:
                        store_rows(u + 1)
            schedule(sp, unit)
            store_out(UNITS - 1, (UNITS - 1) % 2)
            sp.wait_ge(rows_stored, 16 * UNITS)
            sp.wait_ge(out_stored, 16 * UNITS)

        @block.tensor
        def _(pe):
            def project_in(u, i):
                pe.wait_ge(ctx_loaded, 16 * (u + 1))
                wait(pe, dt_read, 2 * u)
                for e in range(2):
                    et = 2 * i + e
                    for c in range(CT):
                        mm = nc.tensor.matmul(ps_misc[i][:, e * L:(e + 1) * L], win[:, c, et * P:(et + 1) * P],
                                              ctxs[:, c, :], start=(c == 0), stop=(c == CT - 1))
                mm.then_inc(proj_done, 1)

            def project_x(u):
                pe.wait_ge(u_ready, u + 1)
                pe.wait_ge(xin_ready, 2 * (u + 1))
                wait(pe, xlow_ready, 2 * (u - 1))
                for et in range(ET):
                    mm = nc.tensor.matmul(ps_misc[0][0:RANK + 2 * NST, 0:L], wx[:, et, :], u2[:, et, :],
                                          start=(et == 0), stop=(et == ET - 1))
                mm.then_inc(xdbl_done, 1)

            def project_dt(u):
                pe.wait_ge(xdbl_ready, u + 1)
                for et in range(ET):
                    mm = nc.tensor.matmul(ps_misc[1 - et // 2][:, (et % 2) * L:(et % 2 + 1) * L],
                                          wdt[:, et * P:(et + 1) * P], xdbl[0:RANK, :], start=True, stop=True)
                    if et % 2 == 1:
                        mm.then_inc(dt_done, 1)

            def transpose_y(u, h):
                pe.wait_ge(yg_ready, u + 1)
                pe.wait_ge(xin_ready, min(2 * (u + 3), 2 * UNITS) if isinstance(u, int) else 2 * (u + 3))
                for t in range(TT):
                    for et in range(ET):
                        mm = nc.tensor.transpose(ps_misc[t][:, et * P:(et + 1) * P], gate[h][:, et, t * P:(t + 1) * P],
                                                 ident[:])
                    mm.then_inc(yt_done, 1)

            def transpose_norm(u, h):
                rows = gate[h][:].rearrange("p e t -> p (e t)").rearrange("p (t d) -> p t d", t=TT)
                for t in range(TT):
                    pe.wait_ge(xh_ready, 2 * u + t + 1)
                    for k in range(DT):
                        mm = nc.tensor.transpose(ps_misc[t][:, k * P:(k + 1) * P], rows[:, t, k * P:(k + 1) * P],
                                                 ident[:])
                    mm.then_inc(xht_done, 1)

            def down(w, tile):
                g = HT * w + tile
                pe.wait_ge(gu_ready, g + 1)
                if tile == 0:
                    wait(pe, out_ready, 2 * w)
                for t in range(TT):
                    mm = nc.tensor.matmul(ps_down[t][:], gu[tile % 4][:, t * P:(t + 1) * P], wd[:, tile, :],
                                          start=(tile == 0), stop=(tile == HT - 1))
                mm.then_inc(down_done, 1)

            def feed(w, h, tile, begins):
                g = HT * w + tile
                if tile == 0:
                    pe.wait_ge(xlow_ready, 2 * (w + 1))
                wait(pe, gu_ready, g - 1)
                pe.wait_ge(wlow_loaded[tile % 2], 16 * (HT // 2 * w + tile // 2 + 1))
                for i in range(2):
                    for k in range(DT):
                        cols = slice((i * DT + k) * P, (i * DT + k + 1) * P)
                        products = ((whigh[:, tile, cols], xhigh[h]), (whigh[:, tile, cols], xlow[h]),
                                    (wlow[tile % 2][:, cols], xhigh[h]))
                        for m, (weights, rows) in enumerate(products):
                            mm = nc.tensor.matmul(ps_gu[tile % 2][:, i * L:(i + 1) * L], weights, rows[:, k, :],
                                                  start=(k == 0 and m == 0), stop=(k == DT - 1 and m == 2))
                mm.then_inc(gateup_done, 1)
                if tile >= 2:
                    down(w, tile - 2)
                elif not begins:
                    down(w - 1, HT - 2 + tile)

            pe.wait_ge(small_loaded, 16 * 8)
            project_in(0, 0)
            project_in(0, 1)
            project_x(0)
            project_dt(0)
            pe.wait_ge(consts_made, 4)

            def unit(b, h, inside):
                u = HALVES * b + h
                prepares, follows = inside or u < UNITS - 1, inside or 0 < u <= UNITS
                for n in range(NST):
                    ffn = feeding(u, inside, n)
                    if prepares and n == 0:
                        project_in(u + 1, 0)
                        project_in(u + 1, 1)
                    if ffn:
                        w, tile = ffn
                        begins = not inside and w == 0
                        if begins and tile == 0:
                            pe.wait_ge(high_made, HT)
                            pe.wait_ge(wd_loaded, 16 * SLOTS)
                        feed(w, 1 - h if n >= LAG else h, tile, begins)
                    if follows and n == 1:
                        transpose_y(u - 1, 1 - h)
                    if follows and n == 4:
                        transpose_norm(u - 1, 1 - h)
                    if prepares and n == 8:
                        project_x(u + 1)
                    if prepares and n == 9:
                        project_dt(u + 1)
            schedule(pe, unit)
            down(UNITS - 1, HT - 2)
            down(UNITS - 1, HT - 1)

        @block.scalar
        def _(act):
            def take_in(u, h):
                wait(act, conv_step, (TAPS - 1) * u)
                nc.scalar.activation(xin[:, :, 0:TAPS - 1], xin[:, :, L:L + TAPS - 1] if h else nohead[:],
                                     ACT.Copy).then_inc(head_ready, 1)
                act.wait_ge(head_ready, u + 1)
                for i in range(2):
                    act.wait_ge(proj_done, 2 * u + i + 1)
                    nc.scalar.activation(xin[:, 2 * i:2 * i + 2, TAPS - 1:],
                                         ps_misc[i][:].rearrange("p (e t) -> p e t", e=2), ACT.Copy).then_inc(xin_ready, 1)

            def start_conv(u):
                act.wait_ge(xin_ready, 2 * (u + 1))
                wait(act, xdbl_done, u)
                wait(act, du_ready, u)
                wait(act, acc_started, u)
                for et in range(ET):
                    a = nc.scalar.activation(u2[:, et, :], xin[:, et, 0:L], ACT.Identity, scale=cw[:, et, 0:1],
                                             bias=cb[:, et:et + 1])
                a.then_inc(conv_started, 1)

            def tanh_u(u):
                act.wait_ge(conv_step, (TAPS - 1) * (u + 1))
                wait(act, delta_ready, u)
                nc.scalar.activation(tmp[:], u2[:], ACT.Tanh, scale=0.5).then_inc(uth_ready, 1)

            def norm_z(u, h, b):
                act.wait_ge(znb_ready, b + 1)
                wait(act, xht_done, 2 * (u - 1))
                if isinstance(u, int) and u == 1:
                    act.wait_ge(low_stored[4], 16 * splits(4))
                for et in range(ET):
                    a = nc.scalar.activation(gate[h][:, et, :], xch[:, et, h * L:(h + 1) * L], ACT.Identity,
                                             scale=zr[:, et:et + 1], bias=znb[:, et:et + 1])
                a.then_inc(z_ready, 1)

            def tanh_z(u, h):
                act.wait_ge(z_ready, u + 1)
                act.wait_ge(u_ready, min(u + 2, UNITS) if isinstance(u, int) else u + 2)
                nc.scalar.activation(tmp[:], gate[h][:], ACT.Tanh, scale=0.5).then_inc(zth_ready, 1)

            def take_rows(u):
                act.wait_ge(xdbl_done, u + 1)
                wait(act, rows_stored, 16 * u)
                wait(act, dt_done, 2 * u)
                nc.scalar.activation(xdbl[:], ps_misc[0][0:RANK + 2 * NST, 0:L], ACT.Copy, scale=0.5).then_inc(xdbl_ready, 1)

            def soften(u, h, i):
                if i == 0:
                    act.wait_ge(u_ready, u + 1)
                    wait(act, zgate_ready, u)
                    if isinstance(u, int) and u == 1:
                        act.wait_ge(low_stored[6], 16 * splits(6))
                act.wait_ge(dt_done, 2 * u + i + 1)
                for e in range(2):
                    et = 2 * i + e
                    src = ps_misc[1 - i][:, e * L:(e + 1) * L]
                    nc.scalar.activation(delta[h][:, et, :], src, ACT.Relu, bias=dtb[:, et:et + 1])
                    a = nc.scalar.activation(tmp[:, et, :], src, ACT.Abs, bias=dtb[:, et:et + 1])
                a.then_inc(dt_read, 1)

            def soften_more(u):
                act.wait_ge(dt_read, 2 * (u + 1))
                nc.scalar.activation(tmp[:], tmp[:], ACT.Exp, scale=-1.0).then_inc(soft_step, 1)
                act.wait_ge(soft_step, 2 * u + 1)
                nc.scalar.activation(tmp[:], tmp[:], ACT.Ln, bias=1.0).then_inc(soft_step, 1)

            def start_acc(u, h):
                act.wait_ge(u_ready, u + 1)
                wait(act, yg_ready, u - 1)
                if isinstance(u, int) and u == 1:
                    act.wait_ge(low_stored[5], 16 * splits(5))
                for et in range(ET):
                    a = nc.scalar.activation(acc[h][:, et, :], u2[:, et, :], ACT.Copy, scale=dhalf[:, et:et + 1])
                a.then_inc(acc_started, 1)

            def decays(u, h, n):
                if n == 0:
                    act.wait_ge(delta_ready, u + 1)
                for i in range(2):
                    wait(act, scanned, 2 * (NST * u + n - 1) + i + 1)
                    for e in range(2):
                        et = 2 * i + e
                        a = nc.scalar.activation(ps_da[i][:, e, 1:], delta[h][:, et, 1:], ACT.Exp,
                                                 scale=decay[:, et, n:n + 1])
                    a.then_inc(decays_ready, 1)

            def first_decays(b):
                act.wait_ge(first_made, b + 1)
                nc.scalar.activation(first[:], first[:], ACT.Exp).then_inc(first_ready, 1)

            def split_high(tile):
                act.wait_ge(raw_loaded[SPLIT_IN[tile]], 16 * (turn(tile) + 1))
                nc.scalar.activation(whigh[:, tile, :], raw[SPLIT_IN[tile]], ACT.Copy).then_inc(high_made, 1)

            def tanh_gate(w, tile, more):
                g = HT * w + tile
                act.wait_ge(gateup_done, g + 1)
                if more:
                    act.dma_start(wlow[tile % 2][:].bitcast(F32), low_parts[(tile + 2) % HT]).then_inc(wlow_loaded[tile % 2], 16)
                wait(act, down_done, g - 3)
                nc.scalar.activation(gu[tile % 4][:], ps_gu[tile % 2][:, 0:L], ACT.Tanh, scale=0.5).then_inc(tanh_ready, 1)

            def norm_y(u, h):
                act.wait_ge(ynb_ready, u + 1)
                act.wait_ge(yt_done, 2 * (u + 1))
                rows = gate[h][:].rearrange("p e t -> p (e t)").rearrange("p (t d) -> p t d", t=TT)
                for t in range(TT):
                    nc.scalar.activation(rows[:, t, :], x2[h][:, t, :], ACT.Identity, scale=yr[:, t:t + 1],
                                         bias=ynb[:, t:t + 1]).then_inc(xh_ready, 1)

            def take_norm(u, h):
                wait(act, gateup_done, HT * (u - 1))
                for t in range(TT):
                    act.wait_ge(xht_done, 2 * u + t + 1)
                    nc.scalar.activation(xhigh[h][:, :, t * P:(t + 1) * P],
                                         ps_misc[t][:].rearrange("p (k l) -> p k l", k=DT), ACT.Copy).then_inc(xht_ready, 1)

            act.wait_ge(small_loaded, 16 * 8)
            nc.scalar.activation(decay[:], decay[:], ACT.Exp).then_inc(decay_made, 1)
            act.wait_ge(decay_made, 1)
            nc.scalar.activation(decay[:], decay[:], ACT.Copy, scale=-1.0).then_inc(decay_made, 1)
            nc.scalar.activation(dhalf[:], dhalf[:], ACT.Copy, scale=0.5).then_inc(decay_made, 1)
            act.wait_ge(zeros_made, 3)
            act.wait_ge(decay_made, 3)
            take_in(0, 0)
            start_conv(0)
            for tile in range(4):
                split_high(tile)
            tanh_u(0)
            for tile in range(4, 8):
                split_high(tile)
            take_rows(0)
            split_high(8)
            split_high(9)
            soften(0, 0, 0)
            soften(0, 0, 1)
            soften_more(0)
            decays(0, 0, 0)
            start_acc(0, 0)

            def unit(b, h, inside):
                u = HALVES * b + h
                scans, prepares = inside or u < UNITS, inside or u < UNITS - 1
                follows = inside or 0 < u <= UNITS
                for n in range(NST):
                    ffn = feeding(u, inside, n)
                    if prepares and n == 0:
                        take_in(u + 1, 1 - h)
                    if ffn:
                        w, tile = ffn
                        tanh_gate(w, tile, inside or w < UNITS - 1 or tile < HT - 2)
                    if not inside and u == 0 and 0 < n < HT - 9:
                        split_high(9 + n)
                    if prepares and n == 1:
                        start_conv(u + 1)
                    if follows and n == 2:
                        norm_y(u - 1, 1 - h)
                    if follows and n == 4:
                        take_norm(u - 1, 1 - h)
                    if prepares and n == 5:
                        tanh_u(u + 1)
                    if scans and n == 7:
                        norm_z(u, h, b)
                    if scans and n == 8:
                        tanh_z(u, h)
                    if prepares and n == 8:
                        take_rows(u + 1)
                    if prepares and n == 9:
                        start_acc(u + 1, 1 - h)
                    if prepares and n in (10, 11):
                        soften(u + 1, 1 - h, n - 10)
                    if prepares and n == 12:
                        soften_more(u + 1)
                    if prepares and h == 0 and n == 15:
                        first_decays(b)
                    if scans and n < NST - 1:
                        decays(u, h, n + 1)
                    elif prepares and n == NST - 1:
                        decays(u + 1, 1 - h, 0)
            schedule(act, unit)

        @block.gpsimd
        def _(pool):
            def rstd_z(b):
                pool.wait_ge(stats_step, 2 * (b + 1))
                wait(pool, z_ready, HALVES * b)
                nc.gpsimd.tensor_tensor(zr[:], zmv[:, :, 1], epsilon[:], ALU.add).then_inc(rstd_step, 1)
                pool.wait_ge(rstd_step, 2 * b + 1)
                nc.gpsimd.tensor_tensor(zr[:], zr[:], neghalf[:], ALU.pow).then_inc(rstd_step, 1)

            def rstd_y(u):
                pool.wait_ge(ystats_step, 2 * (u + 1))
                wait(pool, xh_ready, 2 * u)
                nc.gpsimd.tensor_tensor(yr[:], ymv[:, :, 1], epsilon[:, 0:TT], ALU.add).then_inc(yrstd_step, 1)
                pool.wait_ge(yrstd_step, 2 * u + 1)
                nc.gpsimd.tensor_tensor(yr[:], yr[:], neghalf[:, 0:TT], ALU.pow).then_inc(yrstd_step, 1)

            def split_low(tile):
                pool.wait_ge(raw_loaded[SPLIT_IN[tile]], 16 * (turn(tile) + 1))
                pool.wait_ge(high_made, tile + 1)
                nc.gpsimd.tensor_tensor(raw[SPLIT_IN[tile]].bitcast(F32R), raw[SPLIT_IN[tile]], whigh[:, tile, :].bitcast(F32),
                                        ALU.subtract).then_inc(pool_low_made, 1)

            def scale(u, h, b, n):
                if n % 2 == 0:
                    pool.wait_ge(bc_loaded[n // 2 % 2], 16 * (SLOTS // 2 * u + n // 4 + 1))
                pool.wait_ge(scanned, 2 * (NST * u + n + 1))
                if h == 0:
                    pool.wait_ge(saved, NST * b + n + 1)
                s = st[n % XBUF]
                nc.gpsimd.tensor_tensor(s[:], s[:], bc[n // 2 % 2][:, 1, n % 2:n % 2 + 1, :].broadcast_to([P, ET, L]),
                                        ALU.mult).then_inc(scaled, 1)

            def add_pair(u, jp):
                pool.wait_ge(scaled, NST * u + 2 * jp + 2)
                s = st[2 * jp % XBUF]
                nc.gpsimd.tensor_tensor(s[:], s[:], st[(2 * jp + 1) % XBUF][:], ALU.add).then_inc(paired, 1)

            pool.memset(neghalf[:], -0.5).then_inc(consts_made, 1)
            pool.memset(epsilon[:], EPS).then_inc(consts_made, 1)
            pool.memset(ident[:], 0.0).then_inc(consts_made, 1)
            pool.wait_ge(consts_made, 3)
            pool.affine_select(out=ident[:], in_=ident[:], compare_op=ALU.not_equal, fill=1.0, base=0,
                               pattern=[[-1, P]], channel_multiplier=1).then_inc(consts_made, 1)
            pool.wait_ge(small_loaded, 16 * 8)
            rstd_z(0)
            for tile in POOL_SPLITS:
                split_low(tile)

            def unit(b, h, inside):
                u = HALVES * b + h
                scans, prepares = inside or u < UNITS, inside or u < UNITS - 1
                for jp in range(SLOTS):
                    if scans:
                        scale(u, h, b, 2 * jp)
                    if scans and jp == 2 and h == 0 and (inside or u > 0):
                        rstd_z(b)
                    if scans:
                        scale(u, h, b, 2 * jp + 1)
                    if jp == 0 and (inside or 0 < u <= UNITS):
                        rstd_y(u - 1)
                    if scans:
                        add_pair(u, jp)
                    if not inside and u == 0 and jp < len(POOL_LATE_SPLITS):
                        split_low(POOL_LATE_SPLITS[jp])
            schedule(pool, unit)

        @block.vector
        def _(dve):
            def stats_z(b):
                dve.wait_ge(xch_loaded, 16 * (b + 1))
                wait(dve, znb_ready, b)
                for et in range(ET):
                    i = nc.vector.bn_stats(zst[:, et, :], xch[:, et, :])
                i.then_inc(stats_step, 1)
                dve.wait_ge(stats_step, 2 * b + 1)
                nc.vector.memset(waiter[:], 0.0)
                for et in range(ET):
                    i = nc.vector.bn_aggr(zmv[:, et, :], zst[:, et, :])
                i.then_inc(stats_step, 1)

            def shift_z(b):
                dve.wait_ge(rstd_step, 2 * (b + 1))
                nc.vector.scalar_tensor_tensor(znb[:], zmv[:, :, 0], -1.0, zr[:], ALU.mult, ALU.mult).then_inc(znb_ready, 1)

            def convolve(u, taps):
                for tap in taps:
                    if tap == 1:
                        dve.wait_ge(conv_started, u + 1)
                    else:
                        dve.wait_ge(conv_step, (TAPS - 1) * u + tap - 1)
                    for et in range(ET):
                        i = nc.vector.scalar_tensor_tensor(u2[:, et, :], xin[:, et, tap:tap + L], cw[:, et, tap:tap + 1],
                                                           u2[:, et, :], ALU.mult, ALU.add)
                    i.then_inc(conv_step, 1)

            def silu_u(u):
                dve.wait_ge(uth_ready, u + 1)
                nc.vector.scalar_tensor_tensor(u2[:], tmp[:], 1.0, u2[:], ALU.add, ALU.mult).then_inc(u_ready, 1)

            def split_low(tile):
                dve.wait_ge(raw_loaded[SPLIT_IN[tile]], 16 * (turn(tile) + 1))
                dve.wait_ge(high_made, tile + 1)
                nc.vector.tensor_tensor(raw[SPLIT_IN[tile]].bitcast(F32R), raw[SPLIT_IN[tile]], whigh[:, tile, :].bitcast(F32),
                                        ALU.subtract).then_inc(dve_low_made, 1)

            def silu_z(u, h):
                dve.wait_ge(zth_ready, u + 1)
                nc.vector.scalar_tensor_tensor(gate[h][:], tmp[:], 1.0, gate[h][:], ALU.add, ALU.mult).then_inc(zgate_ready, 1)

            def step_u(u, h):
                dve.wait_ge(soft_step, 2 * (u + 1))
                nc.vector.tensor_tensor(delta[h][:], delta[h][:], tmp[:], ALU.add).then_inc(delta_ready, 1)

            def times_u(u, h):
                dve.wait_ge(delta_ready, u + 1)
                if isinstance(u, int) and u == 1:
                    dve.wait_ge(low_stored[7], 16 * splits(7))
                nc.vector.scalar_tensor_tensor(du[h][:], delta[h][:], 0.5, u2[:], ALU.mult, ALU.mult).then_inc(du_ready, 1)

            def make_first(b):
                dve.wait_ge(delta_ready, HALVES * b + 2)
                for et in range(ET):
                    i = nc.vector.tensor_scalar(first[:, et, :], decay[:, et, :], delta[1][:, et, 0:1], None, ALU.mult)
                i.then_inc(first_made, 1)

            def pass_on(b):
                dve.wait_ge(first_ready, b + 1)
                dve.wait_ge(saved, NST * (b + 1))
                nc.vector.tensor_tensor(passed[:], carry[:], first[:], ALU.mult).then_inc(passed_on, 1)

            def feed_state(u, h, b, n):
                s = st[n % XBUF]
                if isinstance(u, int) and u == 0 and n in (2, 3):
                    dve.wait_ge(low_stored[n], 16 * splits(n))
                if n == 0:
                    dve.wait_ge(du_ready, u + 1)
                if n % 2 == 0:
                    dve.wait_ge(bc_loaded[n // 2 % 2], 16 * (SLOTS // 2 * u + n // 4 + 1))
                    wait(dve, added, SLOTS * u + n // 2 - 1)
                nc.vector.tensor_tensor(s[:], du[h][:], bc[n // 2 % 2][:, 0, n % 2:n % 2 + 1, :].broadcast_to([P, ET, L]),
                                        ALU.mult).then_inc(input_ready, 1)

            def seed(u, b, n):
                s = st[n % XBUF]
                dve.wait_ge(input_ready, NST * u + n + 1)
                dve.wait_ge(passed_on, b + 1)
                nc.vector.tensor_tensor(s[:, :, 0], s[:, :, 0], passed[:, :, n], ALU.add).then_inc(seeded, 1)

            def scan(u, h, b, n):
                dve.wait_ge(input_ready, NST * u + n + 1)
                if h == 1:
                    dve.wait_ge(seeded, NST * b + n + 1)
                for i in range(2):
                    flat = st[n % XBUF][:, 2 * i:2 * i + 2, :].rearrange("p e t -> p (e t)")
                    dve.wait_ge(decays_ready, 2 * (NST * u + n) + i + 1)
                    nc.vector.tensor_tensor_scan(flat, ps_da[i][:].rearrange("p e t -> p (e t)"), flat, 0.0,
                                                 ALU.mult, ALU.add).then_inc(scanned, 1)

            def save(u, b, n):
                dve.wait_ge(scanned, 2 * (NST * u + n + 1))
                nc.vector.tensor_copy(carry[:, :, n], st[n % XBUF][:, :, L - 1]).then_inc(saved, 1)

            def add(u, h, jp):
                if jp == 0:
                    dve.wait_ge(acc_started, u + 1)
                dve.wait_ge(paired, SLOTS * u + jp + 1)
                wait(dve, added, SLOTS * u + jp)
                nc.vector.tensor_tensor(acc[h][:], acc[h][:], st[2 * jp % XBUF][:], ALU.add).then_inc(added, 1)

            def gate_y(u, h):
                dve.wait_ge(added, SLOTS * (u + 1))
                dve.wait_ge(zgate_ready, u + 1)
                nc.vector.scalar_tensor_tensor(gate[h][:], acc[h][:], 0.5, gate[h][:], ALU.mult, ALU.mult).then_inc(yg_ready, 1)

            def add_y(u, h, b):
                dve.wait_ge(x2_loaded[h], 16 * (b + 1))
                for t in range(TT):
                    dve.wait_ge(yt_done, 2 * u + t + 1)
                    nc.vector.tensor_tensor(x2[h][:, t, :], ps_misc[t][:], x2[h][:, t, :], ALU.add).then_inc(x2_ready, 1)
                for t in range(TT):
                    dve.wait_ge(x2_ready, 2 * u + t + 1)
                    i = nc.vector.bn_stats(yst[:, t, :], x2[h][:, t, :])
                i.then_inc(ystats_step, 1)
                dve.wait_ge(ystats_step, 2 * u + 1)
                wait(dve, ynb_ready, u)
                nc.vector.memset(waiter[:], 0.0)
                for t in range(TT):
                    i = nc.vector.bn_aggr(ymv[:, t, :], yst[:, t, :])
                i.then_inc(ystats_step, 1)

            def shift_y(u):
                dve.wait_ge(yrstd_step, 2 * (u + 1))
                nc.vector.scalar_tensor_tensor(ynb[:], ymv[:, :, 0], -1.0, yr[:], ALU.mult, ALU.mult).then_inc(ynb_ready, 1)

            def take_low(u, h):
                wait(dve, gateup_done, HT * (u - 1))
                for t in range(TT):
                    dve.wait_ge(xht_ready, 2 * u + t + 1)
                    nc.vector.tensor_tensor(xlow[h][:, :, t * P:(t + 1) * P],
                                            ps_misc[t][:].rearrange("p (k l) -> p k l", k=DT),
                                            xhigh[h][:, :, t * P:(t + 1) * P].bitcast(F32), ALU.subtract
                                            ).then_inc(xlow_ready, 1)

            def silu_gate(w, tile):
                g = HT * w + tile
                dve.wait_ge(tanh_ready, g + 1)
                nc.vector.scalar_tensor_tensor(gu[tile % 4][:], gu[tile % 4][:], 1.0, ps_gu[tile % 2][:, 0:L],
                                               ALU.add, ALU.mult).then_inc(silu_ready, 1)

            def times_up(w, tile):
                g = HT * w + tile
                dve.wait_ge(silu_ready, g + 1)
                nc.vector.tensor_tensor(gu[tile % 4][:], gu[tile % 4][:], ps_gu[tile % 2][:, L:2 * L], ALU.mult
                                        ).then_inc(gu_ready, 1)

            def finish(w, h):
                dve.wait_ge(down_done, HT * (w + 1))
                for t in range(TT):
                    nc.vector.scalar_tensor_tensor(x2[h][:, t, :], ps_down[t][:], 0.5, x2[h][:, t, :], ALU.mult, ALU.add
                                                   ).then_inc(out_ready, 1)

            nc.vector.memset(nohead[:], 0.0).then_inc(zeros_made, 1)
            for bank in ps_da:
                nc.vector.memset(bank[:, :, 0], 0.0).then_inc(zeros_made, 1)
            stats_z(0)
            shift_z(0)
            dve.wait_ge(small_loaded, 16 * 8)
            convolve(0, range(1, TAPS))
            silu_u(0)
            for tile in DVE_SPLITS:
                split_low(tile)
            step_u(0, 0)
            times_u(0, 0)

            def unit(b, h, inside):
                u = HALVES * b + h
                scans, prepares = inside or u < UNITS, inside or u < UNITS - 1
                follows = inside or 0 < u <= UNITS
                for n in range(NST):
                    ffn = feeding(u, inside, n)
                    if n == LAG + 2 and (inside or 2 <= u <= UNITS):
                        finish(u - 2, h)
                    if scans:
                        feed_state(u, h, b, n)
                        if h == 1 and n == 0:
                            pass_on(b)
                    if ffn:
                        silu_gate(*ffn)
                    if scans and h == 1:
                        seed(u, b, n)
                    if follows and n == 2:
                        shift_y(u - 1)
                    if ffn and h == 1:
                        times_up(*ffn)
                    if scans:
                        scan(u, h, b, n)
                    if ffn and h == 0:
                        times_up(*ffn)
                    if scans and h == 0:
                        save(u, b, n)
                    if not inside and u == 0 and n in (1, 3):
                        split_low(DVE_LATE_SPLITS[n // 2])
                    if follows and n == 0:
                        add(u - 1, 1 - h, SLOTS - 1)
                        gate_y(u - 1, 1 - h)
                    if follows and n == 1:
                        add_y(u - 1, 1 - h, b if h else b - 1)
                    if follows and n == 4:
                        take_low(u - 1, 1 - h)
                    if prepares and 2 <= n < 2 + TAPS - 1:
                        convolve(u + 1, [n - 1])
                    if scans and h == 0 and (inside or u > 0) and n == 3:
                        stats_z(b)
                    if scans and h == 0 and (inside or u > 0) and n == 5:
                        shift_z(b)
                    if prepares and n == 6:
                        silu_u(u + 1)
                    if scans and n == 9:
                        silu_z(u, h)
                    if prepares and n == 12:
                        step_u(u + 1, 1 - h)
                    if prepares and n == 13:
                        times_u(u + 1, 1 - h)
                    if prepares and h == 0 and n == 13:
                        make_first(b)
                    if scans and n > 1 and n % 2 == 1:
                        add(u, h, n // 2 - 1)
            schedule(dve, unit)
            finish(UNITS - 1, (UNITS - 1) % 2)


def program(nc, shapes):
    ins = [nc.dram_tensor(f"in_{name}", shape, F32, kind="ExternalInput").ap() for name, shape in shapes]
    out = nc.dram_tensor("out_0", (BATCH, SEQ, DIM), F32, kind="ExternalOutput").ap()
    build(nc, *ins, out)


def kernel(x, ctx_1024, L0_xattn_in_proj_w, L0_xattn_conv_w, L0_xattn_conv_b, L0_xattn_x_proj_w, L0_xattn_dt_proj_w,
           L0_xattn_dt_proj_b, L0_xattn_A_log, L0_xattn_D, L0_ffn_w_gate, L0_ffn_w_up, L0_ffn_w_down):
    import concourse.bacc as bacc
    from concourse.bass_utils import run_bass_kernel_spmd

    def tiled(a):
        a = np.asarray(a)
        return a.reshape(-1, P, *a.shape[1:]).swapaxes(0, 1)

    ctx = np.asarray(ctx_1024).reshape(UNITS, L, CT, P).transpose(0, 3, 2, 1)
    gate_up = np.stack([np.asarray(L0_ffn_w_gate), np.asarray(L0_ffn_w_up)]).reshape(2, HT, P, DT, P)
    arrays = {
        "ctx": ctx,
        "x": np.asarray(x),
        "w_in": tiled(np.asarray(L0_xattn_in_proj_w).T),
        "conv_w": tiled(L0_xattn_conv_w),
        "conv_b": tiled(L0_xattn_conv_b),
        "w_x": tiled(np.asarray(L0_xattn_x_proj_w).T),
        "w_dt": np.asarray(L0_xattn_dt_proj_w).T,
        "dt_b": tiled(L0_xattn_dt_proj_b),
        "a_log": tiled(L0_xattn_A_log),
        "d_skip": tiled(L0_xattn_D),
        "w_gu": gate_up.transpose(1, 4, 0, 3, 2).reshape(HT, P, GU),
        "w_down": tiled(np.asarray(L0_ffn_w_down).T),
    }
    arrays = {name: np.ascontiguousarray(a) for name, a in arrays.items()}
    nc = bacc.Bacc("TRN2", target_bir_lowering=False, num_devices=1, dynamic_dma_scratch_size=2048)
    program(nc, [(name, a.shape) for name, a in arrays.items()])
    r = run_bass_kernel_spmd(nc, [{f"in_{name}": a for name, a in arrays.items()}], core_ids=[0])
    return np.asarray(r.results[0]["out_0"])
```
